# Optimizing a Trainium2 kernel written in Bass

```python
import numpy as np
import jax
import jax.numpy as jnp

def _softmax(x, axis=-1):
    return jax.nn.softmax(x, axis=axis)

def _gelu(x):
    return jax.nn.gelu(x, approximate=True)

def _silu(x):
    return jax.nn.silu(x)

def _sigmoid(x):
    return jax.nn.sigmoid(x)

def _layernorm(x, axis=-1, eps=1e-05):
    m = jnp.mean(x, axis=axis, keepdims=True)
    v = jnp.var(x, axis=axis, keepdims=True)
    return (x - m) / jnp.sqrt(v + eps)

def _scatter_add(tgt, idx, src, axis=0):
    return tgt.at[idx].add(src)

def _segment_sum(src, seg, n):
    return jax.ops.segment_sum(src, seg, n)
kernel_name = 'mk_sandwich_d1_jaxref_r4_2019e7'

def setup_inputs(seed: int=0):
    np.random.seed(seed)
    _w = jnp.asarray

    def _L0_attn_setup():
        import math
        import jax, jax.numpy as jnp
        import numpy as np
        B, N, D_MODEL, H = (2, 1024, 512, 16)
        HEAD_DIM = D_MODEL // H
        CHUNK = 128

        def _slopes(n_heads):
            start = 2.0 ** (-2.0 ** (-(math.log2(n_heads) - 3)))
            return np.array([start ** (i + 1) for i in range(n_heads)], dtype=np.float32)

        def _lightning_attn(q, k, v):
            b, h, n, d = q.shape
            nc = n // CHUNK
            lam = jnp.exp(-jnp.asarray(_slopes(h)))
            pos = jnp.arange(CHUNK, dtype=jnp.float32)
            decay_q = lam[:, None] ** (pos + 1.0)
            decay_k = lam[:, None] ** (CHUNK - 1.0 - pos)
            diff = pos[:, None] - pos[None, :]
            causal = diff >= 0
            dmask = jnp.where(causal, lam[:, None, None] ** jnp.maximum(diff, 0.0), 0.0)
            lam_c = lam ** CHUNK

            def to_chunks(t):
                return t.reshape(b, h, nc, CHUNK, d).transpose(2, 0, 1, 3, 4)
            qc, kc, vc = (to_chunks(q), to_chunks(k), to_chunks(v))

            def step(S, inp):
                qb, kb, vb = inp
                inter = jnp.einsum('bhcd,bhde->bhce', qb * decay_q[None, :, :, None], S)
                scores = jnp.einsum('bhcd,bhed->bhce', qb, kb) * dmask[None]
                intra = jnp.einsum('bhce,bhed->bhcd', scores, vb)
                S_new = lam_c[None, :, None, None] * S + jnp.einsum('bhcd,bhce->bhde', kb * decay_k[None, :, :, None], vb)
                return (S_new, inter + intra)
            S0 = jnp.zeros((b, h, d, d), dtype=q.dtype)
            _, out = jax.lax.scan(step, S0, (qc, kc, vc))
            return out.transpose(1, 2, 0, 3, 4).reshape(b, h, n, d)
        key = jax.random.key(seed)
        kx, k1, k2, k3, k4 = jax.random.split(key, 5)
        scale = 1.0 / math.sqrt(D_MODEL)
        x = jax.random.normal(kx, (B, N, D_MODEL), dtype=jnp.float32)
        w_qkv = jax.random.normal(k1, (3 * D_MODEL, D_MODEL), dtype=jnp.float32) * scale
        b_qkv = jax.random.normal(k2, (3 * D_MODEL,), dtype=jnp.float32) * 0.01
        w_out = jax.random.normal(k3, (D_MODEL, D_MODEL), dtype=jnp.float32) * scale
        b_out = jax.random.normal(k4, (D_MODEL,), dtype=jnp.float32) * 0.01
        return {'x': x, 'w_qkv': w_qkv, 'b_qkv': b_qkv, 'w_out': w_out, 'b_out': b_out}
    _L0_attn_in = _L0_attn_setup()

    def _L0_ffn_setup():
        import jax, jax.numpy as jnp
        import numpy as np
        E = 8
        TOP_K = 2
        H = 512
        I_MOE = 352
        I_SH = 1408
        B, S = (2, 512)

        def _moe_forward(hidden_states, router_weight, gate_up_proj, down_proj, sh_gate_w, sh_up_w, sh_down_w, shared_gate_w):
            b, s, h = hidden_states.shape
            x = hidden_states.reshape(-1, h)
            shared = jnp.einsum('ti,hi->th', jax.nn.silu(x @ sh_gate_w.T) * (x @ sh_up_w.T), sh_down_w)
            logits = x @ router_weight.T
            probs = jax.nn.softmax(logits.astype(jnp.float32), axis=-1)
            top_v, top_i = jax.lax.top_k(probs, TOP_K)
            top_v = top_v / top_v.sum(axis=-1, keepdims=True)
            combine = (jax.nn.one_hot(top_i, E, dtype=top_v.dtype) * top_v[..., None]).sum(axis=1)
            out = jnp.zeros_like(x)
            for e in range(E):
                gu = x @ gate_up_proj[e].T
                gate, up = (gu[:, :I_MOE], gu[:, I_MOE:])
                cur = jax.nn.silu(gate) * up @ down_proj[e].T
                out = out + cur * combine[:, e:e + 1]
            out = out + jax.nn.sigmoid(x @ shared_gate_w.T) * shared
            return out.reshape(b, s, h)
        key = jax.random.key(seed)
        ks = jax.random.split(key, 8)
        scale = 0.02
        return {'hidden_states': jax.random.normal(ks[0], (B, S, H), dtype=jnp.float32), 'router_weight': jax.random.normal(ks[1], (E, H), dtype=jnp.float32) * scale, 'gate_up_proj': jax.random.normal(ks[2], (E, 2 * I_MOE, H), dtype=jnp.float32) * scale, 'down_proj': jax.random.normal(ks[3], (E, H, I_MOE), dtype=jnp.float32) * scale, 'sh_gate_w': jax.random.normal(ks[4], (I_SH, H), dtype=jnp.float32) * scale, 'sh_up_w': jax.random.normal(ks[5], (I_SH, H), dtype=jnp.float32) * scale, 'sh_down_w': jax.random.normal(ks[6], (H, I_SH), dtype=jnp.float32) * scale, 'shared_gate_w': jax.random.normal(ks[7], (1, H), dtype=jnp.float32) * scale}
    _L0_ffn_in = _L0_ffn_setup()
    _d = {'L0_attn_x': _L0_attn_in['x'], 'L0_attn_w_qkv': _L0_attn_in['w_qkv'], 'L0_attn_b_qkv': _L0_attn_in['b_qkv'], 'L0_attn_w_out': _L0_attn_in['w_out'], 'L0_attn_b_out': _L0_attn_in['b_out'], 'L0_ffn_router_weight': _L0_ffn_in['router_weight'], 'L0_ffn_gate_up_proj': _L0_ffn_in['gate_up_proj'], 'L0_ffn_down_proj': _L0_ffn_in['down_proj'], 'L0_ffn_sh_gate_w': _L0_ffn_in['sh_gate_w'], 'L0_ffn_sh_up_w': _L0_ffn_in['sh_up_w'], 'L0_ffn_sh_down_w': _L0_ffn_in['sh_down_w'], 'L0_ffn_shared_gate_w': _L0_ffn_in['shared_gate_w']}
    _x0 = _d['L0_attn_x']
    _d['L0_attn_x'] = jax.random.normal(jax.random.fold_in(jax.random.key(seed), 1), (4, 1024, 512), dtype=_x0.dtype)
    del _x0
    return _d

def reference(L0_attn_x, L0_attn_w_qkv, L0_attn_b_qkv, L0_attn_w_out, L0_attn_b_out, L0_ffn_router_weight, L0_ffn_gate_up_proj, L0_ffn_down_proj, L0_ffn_sh_gate_w, L0_ffn_sh_up_w, L0_ffn_sh_down_w, L0_ffn_shared_gate_w):

    def _L0_attn_ref(x, w_qkv, b_qkv, w_out, b_out):
        import math
        import jax, jax.numpy as jnp
        import numpy as np
        B, N, D_MODEL, H = (2, 1024, 512, 16)
        HEAD_DIM = D_MODEL // H
        CHUNK = 128

        def _slopes(n_heads):
            start = 2.0 ** (-2.0 ** (-(math.log2(n_heads) - 3)))
            return np.array([start ** (i + 1) for i in range(n_heads)], dtype=np.float32)

        def _lightning_attn(q, k, v):
            b, h, n, d = q.shape
            nc = n // CHUNK
            lam = jnp.exp(-jnp.asarray(_slopes(h)))
            pos = jnp.arange(CHUNK, dtype=jnp.float32)
            decay_q = lam[:, None] ** (pos + 1.0)
            decay_k = lam[:, None] ** (CHUNK - 1.0 - pos)
            diff = pos[:, None] - pos[None, :]
            causal = diff >= 0
            dmask = jnp.where(causal, lam[:, None, None] ** jnp.maximum(diff, 0.0), 0.0)
            lam_c = lam ** CHUNK

            def to_chunks(t):
                return t.reshape(b, h, nc, CHUNK, d).transpose(2, 0, 1, 3, 4)
            qc, kc, vc = (to_chunks(q), to_chunks(k), to_chunks(v))

            def step(S, inp):
                qb, kb, vb = inp
                inter = jnp.einsum('bhcd,bhde->bhce', qb * decay_q[None, :, :, None], S)
                scores = jnp.einsum('bhcd,bhed->bhce', qb, kb) * dmask[None]
                intra = jnp.einsum('bhce,bhed->bhcd', scores, vb)
                S_new = lam_c[None, :, None, None] * S + jnp.einsum('bhcd,bhce->bhde', kb * decay_k[None, :, :, None], vb)
                return (S_new, inter + intra)
            S0 = jnp.zeros((b, h, d, d), dtype=q.dtype)
            _, out = jax.lax.scan(step, S0, (qc, kc, vc))
            return out.transpose(1, 2, 0, 3, 4).reshape(b, h, n, d)
        b, n, dm = x.shape
        qkv = x @ w_qkv.T + b_qkv
        q, k, v = jnp.split(qkv, 3, axis=-1)

        def heads(t):
            return t.reshape(b, n, H, HEAD_DIM).transpose(0, 2, 1, 3)
        attn = _lightning_attn(heads(q), heads(k), heads(v))
        attn = attn.transpose(0, 2, 1, 3).reshape(b, n, dm)
        return attn @ w_out.T + b_out

    def _L0_ffn_ref(hidden_states, router_weight, gate_up_proj, down_proj, sh_gate_w, sh_up_w, sh_down_w, shared_gate_w):
        import jax, jax.numpy as jnp
        import numpy as np
        E = 8
        TOP_K = 2
        H = 512
        I_MOE = 352
        I_SH = 1408
        B, S = (2, 512)

        def _moe_forward(hidden_states, router_weight, gate_up_proj, down_proj, sh_gate_w, sh_up_w, sh_down_w, shared_gate_w):
            b, s, h = hidden_states.shape
            x = hidden_states.reshape(-1, h)
            shared = jnp.einsum('ti,hi->th', jax.nn.silu(x @ sh_gate_w.T) * (x @ sh_up_w.T), sh_down_w)
            logits = x @ router_weight.T
            probs = jax.nn.softmax(logits.astype(jnp.float32), axis=-1)
            top_v, top_i = jax.lax.top_k(probs, TOP_K)
            top_v = top_v / top_v.sum(axis=-1, keepdims=True)
            combine = (jax.nn.one_hot(top_i, E, dtype=top_v.dtype) * top_v[..., None]).sum(axis=1)
            out = jnp.zeros_like(x)
            for e in range(E):
                gu = x @ gate_up_proj[e].T
                gate, up = (gu[:, :I_MOE], gu[:, I_MOE:])
                cur = jax.nn.silu(gate) * up @ down_proj[e].T
                out = out + cur * combine[:, e:e + 1]
            out = out + jax.nn.sigmoid(x @ shared_gate_w.T) * shared
            return out.reshape(b, s, h)
        return _moe_forward(hidden_states, router_weight, gate_up_proj, down_proj, sh_gate_w, sh_up_w, sh_down_w, shared_gate_w)
    x = L0_attn_x
    x = x + _layernorm(_L0_attn_ref(_layernorm(x, axis=-1), L0_attn_w_qkv, L0_attn_b_qkv, L0_attn_w_out, L0_attn_b_out), axis=-1)
    x = x + _layernorm(_L0_ffn_ref(_layernorm(x, axis=-1), L0_ffn_router_weight, L0_ffn_gate_up_proj, L0_ffn_down_proj, L0_ffn_sh_gate_w, L0_ffn_sh_up_w, L0_ffn_sh_down_w, L0_ffn_shared_gate_w), axis=-1)
    return x

_drawn_inputs = setup_inputs


def setup_inputs(seed=0):
    import zlib

    import numpy as np

    out = dict(_drawn_inputs(seed))
    spreads = {}
    factors = {'L0_attn_b_out': 33.228}
    for name, (base, spread) in spreads.items():
        noise = np.random.default_rng([zlib.crc32(name.encode()), seed]).standard_normal(out[name].shape)
        drawn = base * np.exp(spread * noise) if base else spread * noise
        out[name] = jnp.asarray(drawn.astype(out[name].dtype))
    for name, factor in factors.items():
        out[name] = (out[name] * factor).astype(out[name].dtype)
    return out
```

```python
import math
from contextlib import ExitStack

import numpy as np

import concourse.bass as bass
from concourse import mybir

ALU = mybir.AluOpType
ACT = mybir.ActivationFunctionType
F32 = mybir.dt.float32
F32R = mybir.dt.float32r
I32 = mybir.dt.int32
AX = mybir.AxisListType

P = 128
D = 512
KT = D // P
HEADS, HD = 16, 32
GH = P // HD
G = HEADS // GH
TOK = 512
NC = TOK // P
NB = 8
SEQ = 1024
E, I_MOE, I_SH = 8, 352, 1408
NT_SH = I_SH // P
NT = NT_SH + E * I_MOE // P
R = E + 1
EPS = 1e-5
LN_STEPS = 10
FIN_STEPS = 14
RSQRT_GUESS = float(0x5F3759DF)
UNIT = 768
RAW = 3
WSL = 3
NW = 16
WAS = 4


def c_segments(t):
    if t < NT_SH:
        return [(0, 0, P)]
    out, lo = [], (t - NT_SH) * P
    p = 0
    while p < P:
        e = (lo + p) // I_MOE
        end = min(P, (e + 1) * I_MOE - lo)
        limit = {0: P, 32: 32, 64: 64, 96: 32}[p]
        n = min(end - p, limit)
        out.append((1 + e, p, n))
        p += n
    return out


LAST_TILE = {q: max(t for t in range(NT) if any(s[0] == q for s in c_segments(t))) for q in range(R)}


def make_slots():
    s = [[] for _ in range(2 * NT)]
    for c in range(NC):
        s[1 + c].append(("N1", c))
        s[2 + c].append(("T1", c))
    for u in range(4):
        s[2 + u].append(("W", u))
    for m in range(8):
        s[6 + m].append(("QK", m))
        s[7 + m].append(("W", 4 + m))
    for c in range(NC):
        s[15 + c].append(("V", c))
        s[19 + c].append(("W", 12 + c))
    n = 19
    for c in range(NC):
        s[n].append(("KT", c))
        s[n].append(("Z", c, 0))
        seq = [("S", c, 0), ("S", c, 1), ("IP", c, 0), ("S", c, 2), ("S", c, 3), ("IP", c, 1), ("ST", c), ("OUT", c)]
        for i, x in enumerate(seq):
            s[n + 1 + i].append(x)
            if x[0] == "S" and x[2] < G - 1:
                s[n + 1 + i].append(("Z", c, x[2] + 1))
        s[n + 9].append(("L", c))
        s[n + 11].append(("T2", c))
        n += 9
    s[n + 3].append(("R1",))
    s[n + 4].append(("R2",))
    s[n + 4].append(("SM1",))
    s[n + 5].append(("SM2",))
    s[n + 5].append(("SM3",))
    s[n + 6].append(("SM4",))
    s[n + 7].append(("R3",))
    return s


SLOTS = make_slots()
PIECES = [p for slot in SLOTS for p in slot]
PARTS = {"N1": "V", "W": "AV", "T1": "PAV", "QK": "PA", "V": "PV", "KT": "PV", "Z": "A", "S": "PV",
         "IP": "PAV", "ST": "PV", "OUT": "PV", "L": "V", "T2": "PAV", "R1": "PA", "R2": "PV",
         "SM1": "AV", "SM2": "V", "SM3": "V", "SM4": "V", "R3": "PA"}
ORDER = {e: [p for p in PIECES if e in PARTS[p[0]]] for e in "PAV"}
STEPS = {"N1": LN_STEPS, "OUT": LN_STEPS + 1, "L": LN_STEPS + 1, "ST": 2, "SM1": 1, "SM2": 7, "SM3": 5, "SM4": 7}
STEP_BASE, _n = {}, 0
for _p in PIECES:
    STEP_BASE[_p] = _n
    _n += STEPS.get(_p[0], 0)
STEPS_PER_BLOCK = _n


def done(engine, a, *piece):
    return a * len(ORDER[engine]) + ORDER[engine].index(piece) + 1


def build(nc, x, w_att, w_ffn, w_router, b_qk, b_v, b_out, t_mask, t_dq, t_dk, t_lam, t_blk, t_ident, t_rank, t_newton,
          t_keep, out):
    x_d = x.rearrange("(b c p) d -> b c p d", b=NB, c=NC)
    out_d = out.rearrange("(b c p) d -> b c p d", b=NB, c=NC)
    x1_d = nc.dram_tensor("x1_scratch", [NB, NC, P, D], F32, kind="Internal").ap()
    rows_d = nc.dram_tensor("router_scratch", [NB, R, TOK], F32, kind="Internal").ap()

    with ExitStack() as ctx:
        def sb(name, shape, dt=F32):
            return ctx.enter_context(nc.sbuf_tensor(name, [P] + shape, dt))

        def sem(name):
            return ctx.enter_context(nc.semaphore(name))

        mask = sb("decay_mask", [HEADS, P])
        dq = sb("decay_q", [G, P])
        dk = sb("decay_k", [D])
        lam = sb("state_decay", [G, P])
        blk = sb("own_block", [P])
        ident = sb("identity", [P])
        newton = sb("newton", [4])
        rank = sb("rank", [E])
        keep = sb("keep_state", [1], I32)
        bqk = sb("bias_qk", [8])
        bv = sb("bias_v", [D])
        bo = sb("bias_out", [D])
        rw_hi = sb("router_hi", [RWW], F32R)
        rw_lo = sb("router_lo", [RWW], F32R)

        wa_raw = sb("att_w_raw", [2, D])
        wa_hi = sb("att_w_hi", [WAS, D], F32R)
        wa_lo = sb("att_w_lo", [WAS, D], F32R)
        xin = sb("x_in", [2, D])
        xres = sb("x_residual", [2, D])
        xn = sb("x_normed", [D])
        xs_hi = sb("xT_staged_hi", [KT, TOK], F32R)
        xs_lo = sb("xT_staged_lo", [KT, TOK], F32R)
        qT = sb("qT", [G, TOK])
        kT = sb("kT", [G, TOK])
        v = sb("v", [NC, D])
        qz = sb("q_one_head", [2, GH, P])
        qd = sb("q_decayed", [G, P])
        kd = sb("k_decayed", [D])
        probs = sb("probsT", [2, GH, P])
        state = sb("state", [G, P])
        state_new = sb("state_new", [G, P])
        oT_hi = sb("attT_hi", [G, P], F32R)
        oT_lo = sb("attT_lo", [G, P], F32R)
        o = sb("projected", [D])
        rw_raw = o[:, 0:RWW]
        x1 = sb("x1", [2, D])
        st = sb("stats", [6])
        mv = sb("mean_var", [2])
        vs4, rstd, rtmp = sb("var_scaled", [4, 1]), sb("rstd", [1]), sb("rstd_tmp", [1])

        lgT = sb("logitsT", [TOK])
        lg = sb("logits", [NC, R])
        sm = {n: sb("router_" + n, [NC, w]) for n, w in [
            ("max", 1), ("d", E), ("e", E), ("z", 1), ("sum", 1), ("rcp", 1), ("p", E), ("m1", 1), ("m2", 1),
            ("oh", E), ("key", E), ("km", 1), ("oh1", E), ("oh2", E), ("s", 1), ("rs", 1), ("a", E), ("b", E)]}
        comb = sb("combine", [NC, R])

        xt_hi = sb("xT_hi", [KT, TOK], F32R)
        xt_lo = sb("xT_lo", [KT, TOK], F32R)
        raw = sb("ffn_w_raw", [RAW, UNIT])
        w_hi = sb("ffn_w_hi", [WSL, 3 * D], F32R)
        w_lo = sb("ffn_w_lo", [WSL, 3 * D], F32R)
        crow = sb("router_rows", [3, TOK])
        sg = sb("silu_gate", [TOK])
        hid = sb("hidden", [TOK])
        h_hi = sb("hidden_hi", [2, TOK], F32R)
        h_lo = sb("hidden_lo", [2, TOK], F32R)
        x1r = sb("x1_reload", [NC, D])
        fst = sb("fin_stats", [NC, 6])
        fmv = sb("fin_mean_var", [NC, 2])
        fvs = sb("fin_var_scaled", [4, NC])
        frstd, frtmp, fshift = sb("fin_rstd", [NC]), sb("fin_rstd_tmp", [NC]), sb("fin_shift", [NC])

        acc = ctx.enter_context(nc.psum_tensor("ffn_acc", [P, NC, D], F32))
        gate_ps = ctx.enter_context(nc.psum_tensor("gate", [P, TOK], F32))
        up_ps = ctx.enter_context(nc.psum_tensor("up", [P, TOK], F32))
        bank = ctx.enter_context(nc.psum_tensor("piece_banks", [P, 2, D], F32))

        const_in = sem("const_in")
        const_v = sem("const_v")
        const_a = sem("const_a")
        p_piece, a_piece, v_piece = sem("pe_piece"), sem("act_piece"), sem("dve_piece")
        v_step = sem("dve_step")
        passed = sem("wait_passed")
        a_exp = sem("exp_done")
        x_in = [sem(f"x_in{i}") for i in range(2)]
        xres_in = [sem(f"xres_in{i}") for i in range(2)]
        wa_in = [sem(f"att_w_in{i}") for i in range(2)]
        keep_in = sem("keep_in")
        x1_out = [sem(f"x1_out{i}") for i in range(2)]
        rows_out = sem("rows_out")
        row_in = [sem(f"row_in{i}") for i in range(3)]
        raw_in = [sem(f"raw_in{i}") for i in range(RAW)]
        whi_done, wlo_done = sem("whi_done"), sem("wlo_done")
        xt_hi_done, xt_lo_done = sem("xt_hi_done"), sem("xt_lo_done")
        gate_done, up_done, down_done = sem("gate_done"), sem("up_done"), sem("down_done")
        silu_done, gated_done, hid_done = sem("silu_done"), sem("gated_done"), sem("hid_done")
        hhi_done, hlo_done = sem("hhi_done"), sem("hlo_done")
        fin_step = sem("fin_step")
        fin_shift = sem("fin_shift_done")
        out_done = sem("out_done")
        x1r_in = [sem(f"x1r_in{i}") for i in range(NC)]
        out_stored = [sem(f"out_stored{i}") for i in range(NC)]

        def wait(eng, s, value):
            if isinstance(value, int) and value <= 0:
                return
            eng.wait_ge(s, value)

        def bank_of(piece):
            return ORDER["P"].index(piece) % 2

        N_CONST = 12

        def is_first(a):
            return isinstance(a, int) and a == 0

        def settle(eng, a):
            if not isinstance(a, int):
                eng.sem_inc(passed, 1)

        def sp_att_weights(sp, a, u):
            if u >= 2:
                sp.wait_ge(v_piece, done("V", a, "W", u - 2))
            elif not is_first(a):
                sp.wait_ge(v_piece, done("V", a - 1, "W", NW - 2 + u))
            sp.dma_start(out=wa_raw[:, u % 2, :], in_=w_att[u]).then_inc(wa_in[u % 2], 16)

        def sp_slot(sp, a, s):
            if s == 0:
                sp_att_weights(sp, a, 0)
                sp_att_weights(sp, a, 1)
            for piece in SLOTS[s]:
                if piece[0] == "W" and piece[1] + 2 < NW:
                    sp_att_weights(sp, a, piece[1] + 2)

        def sp_raw(sp, f, t, half):
            if t >= NT:
                f, t = f + 1, t - NT
            n = 2 * t + half
            wait(sp, wlo_done, f * 2 * NT + n - RAW + 1)
            sp.dma_start(out=raw[:, n % RAW, :], in_=w_ffn[t, half]).then_inc(raw_in[n % RAW], 16)

        AHEAD = 1

        def sp_body(sp, f, last):
            for t in range(NT):
                if not last:
                    sp_slot(sp, f + 1, 2 * t)
                    sp_slot(sp, f + 1, 2 * t + 1)
                if not (last and t + AHEAD + 1 >= NT):
                    for half in range(2):
                        sp_raw(sp, f, t + AHEAD + 1, half)

        def pool_x(pool, a, c):
            if c >= 2:
                pool.wait_ge(v_piece, done("V", a, "N1", c - 2))
            elif not is_first(a):
                pool.wait_ge(v_piece, done("V", a - 1, "N1", c + 2))
            settle(pool, a)
            pool.dma_start(out=xin[:, c % 2, :], in_=x_d[a, c]).then_inc(x_in[c % 2], 16)

        def pool_xres(pool, a, c):
            if c >= 2:
                pool.wait_ge(v_piece, done("V", a, "L", c - 2))
            elif not is_first(a):
                pool.wait_ge(v_piece, done("V", a - 1, "L", c + 2))
            settle(pool, a)
            pool.dma_start(out=xres[:, c % 2, :], in_=x_d[a, c]).then_inc(xres_in[c % 2], 16)

        def pool_slot(pool, a, s):
            if s == 0:
                pool_x(pool, a, 0)
                pool_x(pool, a, 1)
                if not is_first(a):
                    pool.wait_ge(v_piece, done("V", a - 1, "KT", 0))
                settle(pool, a)
                pool.dma_start(out=keep[:, :], in_=t_keep[a]).then_inc(keep_in, 16)
                pool_xres(pool, a, 0)
                pool_xres(pool, a, 1)
            for piece in SLOTS[s]:
                kind = piece[0]
                if kind == "N1" and piece[1] + 2 < NC:
                    pool_x(pool, a, piece[1] + 2)
                if kind == "L":
                    c = piece[1]
                    pool.wait_ge(v_piece, done("V", a, "L", c))
                    settle(pool, a)
                    pool.dma_start(out=x1_d[a, c], in_=x1[:, c % 2, :]).then_inc(x1_out[c % 2], 16)
                    if c + 2 < NC:
                        pool_xres(pool, a, c + 2)
                if kind == "R3":
                    pool.wait_ge(a_piece, done("A", a, "R3"))
                    settle(pool, a)
                    pool.dma_start(out=rows_d[a], in_=lgT[0:R, :]).then_inc(rows_out, 16)

        def pool_row(pool, f, q):
            pool.wait_ge(rows_out, 16 * (f + 1))
            if q >= 3:
                pool.wait_ge(hid_done, NT * f + LAST_TILE[q - 3] + 1)
            else:
                wait(pool, hid_done, NT * (f - 1) + LAST_TILE[q + R - 3] + 1)
            settle(pool, f)
            row = E if q == 0 else q - 1
            pool.dma_start(out=crow[:, q % 3, :], in_=rows_d[f, row].partition_broadcast(P)).then_inc(row_in[q % 3], 16)

        def pool_body(pool, f, last):
            for t in range(NT):
                if not last:
                    pool_slot(pool, f + 1, 2 * t)
                    pool_slot(pool, f + 1, 2 * t + 1)
                for q in range(3, R):
                    if LAST_TILE[q - 3] == t:
                        pool_row(pool, f, q)
                if t == NT - 4:
                    for c in range(NC):
                        x1_reload(pool, f, c)
            if not last:
                for q in range(3):
                    pool_row(pool, f + 1, q)
            for c in range(NC):
                pool.wait_ge(out_done, NC * f + c + 1)
                settle(pool, f)
                pool.dma_start(out=out_d[f, c], in_=x1r[:, c, :]).then_inc(out_stored[c], 16)

        def x1_reload(pool, f, c):
            pool.wait_ge(x1_out[c % 2], 16 * (NC // 2) * (f + 1))
            wait(pool, out_stored[c], 16 * f)
            settle(pool, f)
            pool.dma_start(out=x1r[:, c, :], in_=x1_d[f, c]).then_inc(x1r_in[c], 16)

        def three(pe, out_ap, l_hi, l_lo, r_hi, r_lo, start, stop):
            pe.matmul(out_ap, l_hi, r_hi, start=start, stop=False)
            pe.matmul(out_ap, l_hi, r_lo, start=False, stop=False)
            return pe.matmul(out_ap, l_lo, r_hi, start=False, stop=stop)

        def pe_piece(pe, a, piece):
            kind = piece[0]
            b = bank[:, bank_of(piece), :]
            i = ORDER["P"].index(piece)
            if i >= 2:
                old = ORDER["P"][i - 2]
                if "A" in PARTS[old[0]]:
                    pe.wait_ge(a_piece, done("A", a, *old))
                if "V" in PARTS[old[0]]:
                    pe.wait_ge(v_piece, done("V", a, *old))
            else:
                wait(pe, a_piece, a * len(ORDER["A"]))
                wait(pe, v_piece, a * len(ORDER["V"]))
            if kind in ("T1", "T2"):
                c = piece[1]
                pe.wait_ge(v_piece, done("V", a, "N1" if kind == "T1" else "L", c))
                for k in range(KT):
                    mm = pe.transpose(b[:, k * P:(k + 1) * P], xn[:, k * P:(k + 1) * P], ident[:, :])
            elif kind == "QK":
                m = piece[1]
                pe.wait_ge(a_piece, done("A", a, "W", m))
                pe.wait_ge(v_piece, done("V", a, "W", m))
                if m == 0:
                    pe.wait_ge(v_piece, done("V", a, "T1", NC - 1))
                for k in range(KT):
                    ks = slice(k * P, (k + 1) * P)
                    mm = three(pe, b, wa_hi[:, m % WAS, ks], wa_lo[:, m % WAS, ks], xs_hi[:, k, :], xs_lo[:, k, :],
                               k == 0, k == KT - 1)
            elif kind == "V":
                c = piece[1]
                cs = slice(c * P, (c + 1) * P)
                if c == 0:
                    pe.wait_ge(a_piece, done("A", a, "W", 11))
                    pe.wait_ge(v_piece, done("V", a, "W", 11))
                for k in range(KT):
                    mm = three(pe, b, xs_hi[:, k, cs], xs_lo[:, k, cs], wa_hi[:, k, :], wa_lo[:, k, :],
                               k == 0, k == KT - 1)
            elif kind == "KT":
                c = piece[1]
                if c == 0:
                    pe.wait_ge(a_piece, done("A", a, "QK", 7))
                for g in range(G):
                    mm = pe.transpose(b[:, g * P:(g + 1) * P], kT[:, g, c * P:(c + 1) * P], ident[:, :])
            elif kind == "S":
                c, g = piece[1:]
                pe.wait_ge(a_piece, done("A", a, "Z", c, g))
                mm = pe.matmul(b, kT[:, g, c * P:(c + 1) * P], qz[:, g % 2].rearrange("p h t -> p (h t)"),
                               start=True, stop=True)
            elif kind == "IP":
                c, half = piece[1:]
                pe.wait_ge(v_piece, done("V", a, "S", c, 2 * half + 1))
                for gl in range(2):
                    g = 2 * half + gl
                    cols = slice(gl * P, (gl + 1) * P)
                    pe.matmul(b[:, cols], state[:, g, :], qd[:, g, :], start=(gl == 0), stop=False,
                              skip_group_check=True)
                    for j in range(GH):
                        r = slice(j * HD, (j + 1) * HD)
                        mm = pe.matmul(b[r, cols], v[:, c, g * P + j * HD:g * P + (j + 1) * HD],
                                       probs[:, g % 2, j, :], start=False, stop=(gl == 1), skip_group_check=True)
            elif kind == "ST":
                c = piece[1]
                for g in range(G):
                    gs = slice(g * P, (g + 1) * P)
                    mm = pe.matmul(b[:, gs], kd[:, gs], v[:, c, gs], start=True, stop=True)
            elif kind == "OUT":
                c = piece[1]
                if c == 0:
                    pe.wait_ge(a_piece, done("A", a, "W", 15))
                    pe.wait_ge(v_piece, done("V", a, "W", 15))
                pe.wait_ge(v_piece, done("V", a, "IP", c, 1))
                for k in range(KT):
                    mm = three(pe, b, oT_hi[:, k, :], oT_lo[:, k, :], wa_hi[:, k, :], wa_lo[:, k, :],
                               k == 0, k == KT - 1)
            elif kind == "R1":
                pe.wait_ge(v_piece, done("V", a, "T2", NC - 1))
                for k in range(KT):
                    ks = slice(k * R, k * R + P)
                    mm = three(pe, b, rw_hi[:, ks], rw_lo[:, ks], xs_hi[:, k, :], xs_lo[:, k, :],
                               k == 0, k == KT - 1)
            elif kind == "R2":
                pe.wait_ge(a_piece, done("A", a, "R1"))
                for c in range(NC):
                    mm = pe.matmul(b[:, c * R:(c + 1) * R], lgT[0:R, c * P:(c + 1) * P], ident[0:R, 0:R],
                                   start=True, stop=True)
            elif kind == "R3":
                pe.wait_ge(v_piece, done("V", a, "SM4"))
                for c in range(NC):
                    mm = pe.matmul(b[0:R, c * P:(c + 1) * P], comb[:, c, :], ident[:, :], start=True, stop=True)
            mm.then_inc(p_piece, 1)

        def pe_slot(pe, a, s):
            for piece in SLOTS[s]:
                if "P" in PARTS[piece[0]]:
                    pe_piece(pe, a, piece)

        def pe_gate_up(pe, f, t):
            n = NT * f + t
            pe.wait_ge(whi_done, 2 * (n + 1))
            pe.wait_ge(wlo_done, 2 * (n + 1))
            if t == 0:
                pe.wait_ge(xt_hi_done, f + 1)
                pe.wait_ge(xt_lo_done, f + 1)
            wait(pe, silu_done, n)
            for part, dst, signal in ((0, gate_ps, gate_done), (1, up_ps, up_done)):
                if part:
                    wait(pe, gated_done, n)
                for k in range(KT):
                    ks = slice(part * D + k * P, part * D + (k + 1) * P)
                    mm = three(pe, dst[:, :], w_hi[:, t % WSL, ks], w_lo[:, t % WSL, ks], xt_hi[:, k, :],
                               xt_lo[:, k, :], k == 0, k == KT - 1)
                mm.then_inc(signal, 1)

        def pe_down(pe, f, t):
            n = NT * f + t
            pe.wait_ge(hhi_done, n + 1)
            pe.wait_ge(hlo_done, n + 1)
            down = slice(2 * D, 3 * D)
            for c in range(NC):
                cs = slice(c * P, (c + 1) * P)
                if t == 0 and c == 0:
                    wait(pe, out_done, NC * f)
                mm = three(pe, acc[:, c, :], h_hi[:, t % 2, cs], h_lo[:, t % 2, cs], w_hi[:, t % WSL, down],
                           w_lo[:, t % WSL, down], t == 0, t == NT - 1)
            mm.then_inc(down_done, 1)

        def pe_body(pe, f, last):
            for t in range(NT):
                pe_gate_up(pe, f, t)
                if not last:
                    pe_slot(pe, f + 1, 2 * t)
                if t:
                    pe_down(pe, f, t - 1)
                if not last:
                    pe_slot(pe, f + 1, 2 * t + 1)
            pe_down(pe, f, NT - 1)

        def chunked(b):
            return b.rearrange("p (k t) -> p k t", t=P)

        def act_piece(act, a, piece):
            kind = piece[0]
            if "P" in PARTS[kind]:
                b = bank[:, bank_of(piece), :]
                act.wait_ge(p_piece, done("P", a, *piece))
            if kind in ("T1", "T2"):
                c = piece[1]
                op = act.copy(xs_hi[:, :, c * P:(c + 1) * P], chunked(b))
            elif kind == "W":
                u = piece[1]
                act.wait_ge(wa_in[u % 2], 16 * (a * (NW // 2) + u // 2 + 1))
                if u >= 12:
                    act.wait_ge(p_piece, done("P", a, "V", NC - 1))
                elif u >= WAS:
                    act.wait_ge(p_piece, done("P", a, "QK", u - WAS))
                else:
                    wait(act, p_piece, a * len(ORDER["P"]))
                op = act.copy(wa_hi[:, u % WAS, :], wa_raw[:, u % 2, :])
            elif kind == "QK":
                m = piece[1]
                dst = qT if m < G else kT
                op = act.activation(dst[:, m % G, :], b, ACT.Identity, bias=bqk[:, m:m + 1])
            elif kind == "Z":
                c, g = piece[1:]
                if (c, g) == (0, 0):
                    act.wait_ge(a_piece, done("A", a, "QK", G - 1))
                if 4 * c + g >= 2:
                    cc, gg = divmod(4 * c + g - 2, G)
                    act.wait_ge(p_piece, done("P", a, "S", cc, gg))
                for j in range(GH):
                    r = slice(j * HD, (j + 1) * HD)
                    op = act.copy(qz[r, g % 2, j, :], qT[r, g, c * P:(c + 1) * P])
            elif kind == "IP":
                c, half = piece[1:]
                if half == 0 and c > 0:
                    act.wait_ge(p_piece, done("P", a, "OUT", c - 1))
                op = act.copy(oT_hi[:, 2 * half:2 * half + 2, :], chunked(b[:, 0:2 * P]))
            elif kind == "R1":
                wait(act, rows_out, 16 * a)
                op = act.copy(lgT[0:R, :], b[0:R, :])
            elif kind == "SM1":
                act.wait_ge(v_piece, done("V", a, "SM1"))
                act.activation(sm["z"][:, :, :], lg[:, :, E:R], ACT.Exp, scale=-1.0)
                op = act.activation(sm["e"][:, :, :], sm["d"][:, :, :], ACT.Exp)
            elif kind == "R3":
                op = act.copy(lgT[0:R, :], b[0:R, :])
            op.then_inc(a_piece, 1)

        def act_slot(act, a, s):
            for piece in SLOTS[s]:
                if "A" in PARTS[piece[0]]:
                    act_piece(act, a, piece)

        def split_wait(eng, f, t, half):
            n = 2 * t + half
            eng.wait_ge(raw_in[n % RAW], 16 * (f * (2 * NT // RAW) + n // RAW + 1))
            if half == 0:
                wait(eng, down_done, NT * f + t - WSL + 1)

        def act_split(act, f, t):
            if t >= NT:
                f, t = f + 1, t - NT
            for half in range(2):
                split_wait(act, f, t, half)
                us = slice(half * UNIT, (half + 1) * UNIT)
                act.copy(w_hi[:, t % WSL, us], raw[:, (2 * t + half) % RAW, :]).then_inc(whi_done, 1)

        def act_xt(act, f):
            wait(act, up_done, NT * f)
            act.wait_ge(a_piece, done("A", f, "T2", NC - 1))
            act.copy(xt_hi[:, :, :], xs_hi[:, :, :].bitcast(F32)).then_inc(xt_hi_done, 1)

        def act_fin(act, f):
            act.wait_ge(fin_step, FIN_STEPS * (f + 1))
            for c in range(NC):
                act.wait_ge(x1r_in[c], 16 * (f + 1))
                act.activation(x1r[:, c, :], x1r[:, c, :], ACT.Identity,
                               bias=fshift[:, c:c + 1]).then_inc(fin_shift, 1)

        def act_body(act, f, last):
            for t in range(NT):
                n = NT * f + t
                act.wait_ge(gate_done, n + 1)
                wait(act, gated_done, n)
                act.activation(sg[:, :], gate_ps[:, :], ACT.Silu).then_inc(silu_done, 1)
                if t and t + AHEAD < NT or t == NT - 1 and not last:
                    act_split(act, f, t + AHEAD)
                act.wait_ge(hid_done, n + 1)
                wait(act, down_done, NT * f + t - 1 if t >= 2 else NT * f)
                act.copy(h_hi[:, t % 2, :], hid[:, :]).then_inc(hhi_done, 1)
                if not last:
                    act_slot(act, f + 1, 2 * t)
                    act_slot(act, f + 1, 2 * t + 1)
            if not last:
                act_xt(act, f + 1)
                act_split(act, f + 1, 1)
            act_fin(act, f)

        def rsqrt(ve, var, n, vs, y, t, chain):
            chain(ve.scalar_tensor_tensor(out=vs[:, :, :], in0=var.unsqueeze(1).to_broadcast([P, 4, n]), scalar=EPS,
                                          in1=newton[:, :].unsqueeze(2).to_broadcast([P, 4, n]), op0=ALU.add,
                                          op1=ALU.mult))
            chain(ve.tensor_scalar(y[:, :].bitcast(I32), vs[:, 0, :].bitcast(I32), -0.5, RSQRT_GUESS, ALU.mult,
                                   ALU.add))
            for i in range(3):
                if n == 1:
                    chain(ve.scalar_tensor_tensor(out=t[:, :], in0=y[:, :], scalar=vs[:, i + 1, 0:1], in1=y[:, :],
                                                  op0=ALU.mult, op1=ALU.mult))
                else:
                    chain(ve.tensor_tensor(t[:, :], y[:, :], y[:, :], ALU.mult))
                    chain(ve.tensor_tensor(t[:, :], t[:, :], vs[:, i + 1, :], ALU.mult))
                chain(ve.scalar_tensor_tensor(out=y[:, :], in0=t[:, :], scalar=3.0, in1=y[:, :], op0=ALU.add,
                                              op1=ALU.mult))

        def chained(eng, sem_, base):
            count = [0]

            def chain(op):
                count[0] += 1
                op.then_inc(sem_, 1)
                eng.wait_ge(sem_, base + count[0])
            return chain

        def layernorm(ve, src, dst, a, piece, n0):
            chain = chained(ve, v_step, a * STEPS_PER_BLOCK + STEP_BASE[piece] + n0)
            chain(ve.bn_stats(st[:, :], src))
            settle(ve, a)
            chain(ve.bn_aggr(mv[:, :], st[:, :]))
            rsqrt(ve, mv[:, 1:2], 1, vs4, rstd, rtmp, chain)
            return ve.tensor_scalar(dst, src, mv[:, 0:1], rstd[:, 0:1], ALU.subtract, ALU.mult)

        def dve_piece(ve, a, piece):
            kind = piece[0]
            if "P" in PARTS[kind]:
                b = bank[:, bank_of(piece), :]
                ve.wait_ge(p_piece, done("P", a, *piece))

            def step(op, n):
                op.then_inc(v_step, 1)
                ve.wait_ge(v_step, a * STEPS_PER_BLOCK + STEP_BASE[piece] + n)

            if kind == "N1":
                c = piece[1]
                ve.wait_ge(x_in[c % 2], 16 * (a * (NC // 2) + c // 2 + 1))
                if c:
                    ve.wait_ge(p_piece, done("P", a, "T1", c - 1))
                op = layernorm(ve, xin[:, c % 2, :], xn[:, :], a, piece, 0)
            elif kind in ("T1", "T2"):
                c = piece[1]
                cs = slice(c * P, (c + 1) * P)
                ve.wait_ge(a_piece, done("A", a, *piece))
                op = ve.tensor_tensor(xs_lo[:, :, cs], chunked(b), xs_hi[:, :, cs].bitcast(F32), ALU.subtract)
            elif kind == "W":
                u = piece[1]
                ve.wait_ge(a_piece, done("A", a, *piece))
                op = ve.tensor_tensor(wa_lo[:, u % WAS, :], wa_raw[:, u % 2, :], wa_hi[:, u % WAS, :].bitcast(F32),
                                      ALU.subtract)
            elif kind == "V":
                op = ve.tensor_tensor(v[:, piece[1], :], b, bv[:, :], ALU.add)
            elif kind == "KT":
                c = piece[1]
                if c == 0:
                    ve.wait_ge(keep_in, 16 * (a + 1))
                    wait(ve, v_piece, (a - 1) * len(ORDER["V"]) + ORDER["V"].index(("ST", NC - 1)) + 1
                         if not isinstance(a, int) or a > 0 else 0)
                    s_flat = state[:, :, :].rearrange("p g d -> p (g d)").bitcast(I32)
                    ve.tensor_tensor(s_flat, s_flat, keep[:, :].to_broadcast([P, D]), ALU.bitwise_and)
                    ve.wait_ge(a_piece, done("A", a, "QK", G - 1))
                ve.tensor_tensor(qd[:, :, :], qT[:, :, c * P:(c + 1) * P], dq[:, :, :], ALU.mult)
                op = ve.tensor_tensor(kd[:, :], b, dk[:, :], ALU.mult)
            elif kind == "S":
                c, g = piece[1:]
                op = ve.tensor_tensor(probs[:, g % 2, :, :], chunked(b), mask[:, GH * g:GH * (g + 1), :], ALU.mult)
            elif kind == "IP":
                c, half = piece[1:]
                gs = slice(2 * half, 2 * half + 2)
                ve.wait_ge(a_piece, done("A", a, *piece))
                op = ve.tensor_tensor(oT_lo[:, gs, :], chunked(b[:, 0:2 * P]), oT_hi[:, gs, :].bitcast(F32),
                                      ALU.subtract)
            elif kind == "ST":
                ve.tensor_tensor(state_new[:, :, :], chunked(b), blk[:, :].unsqueeze(1).to_broadcast([P, G, P]),
                                 ALU.mult).then_inc(v_step, 1)
                step(ve.tensor_tensor(state[:, :, :], state[:, :, :], lam[:, :, :], ALU.mult), 2)
                op = ve.tensor_tensor(state[:, :, :], state[:, :, :], state_new[:, :, :], ALU.add)
            elif kind == "OUT":
                step(ve.tensor_tensor(o[:, :], b, bo[:, :], ALU.add), 1)
                op = layernorm(ve, o[:, :], o[:, :], a, piece, 1)
            elif kind == "L":
                c = piece[1]
                n = a * (NC // 2) + c // 2
                ve.wait_ge(xres_in[c % 2], 16 * (n + 1))
                wait(ve, x1_out[c % 2], 16 * n)
                ve.wait_ge(v_piece, done("V", a, "OUT", c))
                step(ve.tensor_tensor(x1[:, c % 2, :], o[:, :], xres[:, c % 2, :], ALU.add), 1)
                if c:
                    ve.wait_ge(p_piece, done("P", a, "T2", c - 1))
                op = layernorm(ve, x1[:, c % 2, :], xn[:, :], a, piece, 1)
            elif kind == "R2":
                op = ve.tensor_copy(lg[:, :, :], b[:, 0:NC * R].rearrange("p (c r) -> p c r", r=R))
            elif kind == "SM1":
                ve.wait_ge(v_piece, done("V", a, "R2"))
                l8 = lg[:, :, 0:E]
                step(ve.tensor_reduce(sm["max"][:, :, :], l8, AX.X, ALU.max), 1)
                op = ve.tensor_tensor(sm["d"][:, :, :], l8, wide(sm["max"]), ALU.subtract)
            elif kind == "SM2":
                ve.wait_ge(a_piece, done("A", a, "SM1"))
                step(ve.tensor_reduce(sm["sum"][:, :, :], sm["e"][:, :, :], AX.X, ALU.add), 1)
                step(ve.reciprocal(sm["rcp"][:, :, :], sm["sum"][:, :, :]), 2)
                step(ve.tensor_tensor(sm["p"][:, :, :], sm["e"][:, :, :], wide(sm["rcp"]), ALU.mult), 3)
                op = first_of_largest(ve, step, 3, "p", "m1", "oh1")
            elif kind == "SM3":
                ve.wait_ge(v_piece, done("V", a, "SM2"))
                step(ve.scalar_tensor_tensor(out=sm["d"][:, :, :], in0=sm["oh1"][:, :, :], scalar=-4.0,
                                             in1=sm["p"][:, :, :], op0=ALU.mult, op1=ALU.add), 1)
                op = first_of_largest(ve, step, 1, "d", "m2", "oh2")
            elif kind == "SM4":
                ve.wait_ge(v_piece, done("V", a, "SM3"))
                step(ve.tensor_tensor(sm["s"][:, :, :], sm["m1"][:, :, :], sm["m2"][:, :, :], ALU.add), 1)
                step(ve.reciprocal(sm["rs"][:, :, :], sm["s"][:, :, :]), 2)
                step(ve.tensor_tensor(sm["a"][:, :, :], sm["oh1"][:, :, :], wide(sm["m1"]), ALU.mult), 3)
                step(ve.tensor_tensor(sm["b"][:, :, :], sm["oh2"][:, :, :], wide(sm["m2"]), ALU.mult), 4)
                step(ve.tensor_tensor(sm["a"][:, :, :], sm["a"][:, :, :], sm["b"][:, :, :], ALU.add), 5)
                step(ve.tensor_tensor(comb[:, :, 0:E], sm["a"][:, :, :], wide(sm["rs"]), ALU.mult), 6)
                step(ve.tensor_scalar(sm["s"][:, :, :], sm["z"][:, :, :], 1.0, None, ALU.add), 7)
                op = ve.reciprocal(comb[:, :, E:R], sm["s"][:, :, :])
            op.then_inc(v_piece, 1)

        def wide(t):
            return t[:, :, :].to_broadcast([P, NC, E])

        def first_of_largest(ve, step, n, src, largest, onehot):
            step(ve.tensor_reduce(sm[largest][:, :, :], sm[src][:, :, :], AX.X, ALU.max), n + 1)
            step(ve.tensor_tensor(sm["oh"][:, :, :], sm[src][:, :, :], wide(sm[largest]), ALU.is_equal), n + 2)
            step(ve.tensor_tensor(sm["key"][:, :, :], sm["oh"][:, :, :],
                                  rank[:, :].unsqueeze(1).to_broadcast([P, NC, E]), ALU.mult), n + 3)
            step(ve.tensor_reduce(sm["km"][:, :, :], sm["key"][:, :, :], AX.X, ALU.max), n + 4)
            return ve.tensor_tensor(sm[onehot][:, :, :], sm["key"][:, :, :], wide(sm["km"]), ALU.is_equal)

        def dve_slot(ve, a, s):
            for piece in SLOTS[s]:
                if "V" in PARTS[piece[0]]:
                    dve_piece(ve, a, piece)

        def dve_split(ve, f, t):
            if t >= NT:
                f, t = f + 1, t - NT
            for half in range(2):
                us = slice(half * UNIT, (half + 1) * UNIT)
                ve.wait_ge(whi_done, f * 2 * NT + 2 * t + half + 1)
                ve.tensor_tensor(w_lo[:, t % WSL, us], raw[:, (2 * t + half) % RAW, :],
                                 w_hi[:, t % WSL, us].bitcast(F32), ALU.subtract).then_inc(wlo_done, 1)

        def dve_xt(ve, f):
            wait(ve, up_done, NT * f)
            ve.wait_ge(v_piece, done("V", f, "T2", NC - 1))
            ve.tensor_copy(xt_lo[:, :, :], xs_lo[:, :, :].bitcast(F32)).then_inc(xt_lo_done, 1)

        def dve_fin_stats(ve, f):
            ve.wait_ge(down_done, NT * (f + 1))
            chain = chained(ve, fin_step, FIN_STEPS * f)
            for c in range(NC):
                op = ve.bn_stats(fst[:, c, :], acc[:, c, :])
            chain(op)
            settle(ve, f)
            for c in range(NC):
                op = ve.bn_aggr(fmv[:, c, :], fst[:, c, :])
            chain(op)
            rsqrt(ve, fmv[:, :, 1], NC, fvs, frstd, frtmp, chain)
            chain(ve.scalar_tensor_tensor(out=fshift[:, :], in0=fmv[:, :, 0], scalar=-1.0, in1=frstd[:, :],
                                          op0=ALU.mult, op1=ALU.mult))

        def dve_fin_out(ve, f):
            for c in range(NC):
                ve.wait_ge(fin_shift, NC * f + c + 1)
                ve.scalar_tensor_tensor(out=x1r[:, c, :], in0=acc[:, c, :], scalar=frstd[:, c:c + 1],
                                        in1=x1r[:, c, :], op0=ALU.mult, op1=ALU.add).then_inc(out_done, 1)

        def dve_body(ve, f, last):
            for t in range(NT):
                n = NT * f + t
                if t and t + AHEAD < NT or t == NT - 1 and not last:
                    dve_split(ve, f, t + AHEAD)
                ve.wait_ge(silu_done, n + 1)
                ve.wait_ge(up_done, n + 1)
                wait(ve, hlo_done, n)
                ve.tensor_tensor(hid[:, :], up_ps[:, :], sg[:, :], ALU.mult).then_inc(gated_done, 1)
                ve.wait_ge(gated_done, n + 1)
                segs = c_segments(t)
                for q in sorted({s[0] for s in segs}):
                    ve.wait_ge(row_in[q % 3], 16 * (f * (R // 3) + q // 3 + 1))
                for q, p0, np_ in segs:
                    r = slice(p0, p0 + np_)
                    op = ve.tensor_tensor(hid[r, :], hid[r, :], crow[r, q % 3, :], ALU.mult)
                op.then_inc(hid_done, 1)
                if not last:
                    dve_slot(ve, f + 1, 2 * t)
                ve.wait_ge(hhi_done, n + 1)
                ve.tensor_tensor(h_lo[:, t % 2, :], hid[:, :], h_hi[:, t % 2, :].bitcast(F32),
                                 ALU.subtract).then_inc(hlo_done, 1)
                if not last:
                    dve_slot(ve, f + 1, 2 * t + 1)
            if not last:
                dve_xt(ve, f + 1)
                dve_split(ve, f + 1, 1)
            dve_fin_stats(ve, f)
            dve_fin_out(ve, f)

        block = ctx.enter_context(nc.Block())

        @block.sync
        def _(sp):
            for dst, src in ((mask, t_mask), (dq, t_dq), (dk, t_dk), (lam, t_lam), (blk, t_blk), (ident, t_ident),
                             (rank, t_rank), (newton, t_newton), (bqk, b_qk)):
                sp.dma_start(out=dst[tuple([slice(None)] * len(dst.shape))], in_=src).then_inc(const_in, 16)
            sp.dma_start(out=rw_raw, in_=w_router).then_inc(const_in, 16)
            sp.dma_start(out=bv[:, :], in_=b_v.partition_broadcast(P)).then_inc(const_in, 16)
            sp.dma_start(out=bo[:, :], in_=b_out.partition_broadcast(P)).then_inc(const_in, 16)
            for half in (0, 1, 2):
                sp_raw(sp, 0, half // 2, half % 2)
            for s in range(2 * NT):
                sp_slot(sp, 0, s)
            sp_raw(sp, 0, 1, 1)
            with sp.Fori(0, NB - 1) as f:
                sp_body(sp, f, False)
            sp_body(sp, NB - 1, True)

        @block.gpsimd
        def _(pool):
            for s in range(2 * NT):
                pool_slot(pool, 0, s)
            for q in range(3):
                pool_row(pool, 0, q)
            with pool.Fori(0, NB - 1) as f:
                pool_body(pool, f, False)
            pool_body(pool, NB - 1, True)
            for c in range(NC):
                pool.wait_ge(out_stored[c], 16 * NB)
            for i in range(2):
                pool.wait_ge(x1_out[i], 16 * NB * NC // 2)
            pool.wait_ge(rows_out, 16 * NB)

        @block.tensor
        def _(pe):
            pe.wait_ge(const_v, 5)
            pe.wait_ge(const_a, 1)
            for s in range(2 * NT):
                pe_slot(pe, 0, s)
            with pe.Fori(0, NB - 1) as f:
                pe_body(pe, f, False)
            pe_body(pe, NB - 1, True)

        @block.scalar
        def _(act):
            act.wait_ge(const_in, 16 * N_CONST)
            act.wait_ge(const_v, 4)
            act.copy(rw_hi[:, :], rw_raw).then_inc(const_a, 1)
            for s in range(2 * NT):
                act_slot(act, 0, s)
            for t in range(2):
                act_split(act, 0, t)
            act_xt(act, 0)
            with act.Fori(0, NB - 1) as f:
                act_body(act, f, False)
            act_body(act, NB - 1, True)

        @block.vector
        def _(ve):
            ve.memset(qz[:, :, :, :], 0.0).then_inc(const_v, 1)
            ve.memset(state[:, :, :], 0.0).then_inc(const_v, 1)
            ve.memset(sg[:, :], 0.0).then_inc(const_v, 1)
            ve.memset(lgT[:, :], 0.0).then_inc(const_v, 1)
            ve.wait_ge(const_in, 16 * N_CONST)
            ve.wait_ge(const_v, 4)
            ve.wait_ge(const_a, 1)
            ve.tensor_tensor(rw_lo[:, :], rw_raw, rw_hi[:, :].bitcast(F32), ALU.subtract).then_inc(const_v, 1)
            for s in range(2 * NT):
                dve_slot(ve, 0, s)
            for t in range(2):
                dve_split(ve, 0, t)
            dve_xt(ve, 0)
            with ve.Fori(0, NB - 1) as f:
                dve_body(ve, f, False)
            dve_body(ve, NB - 1, True)


RWW = (KT - 1) * R + P


def decay_tables():
    start = 2.0 ** (-2.0 ** (-(math.log2(HEADS) - 3)))
    slope = np.array([start ** (i + 1) for i in range(HEADS)], np.float32).astype(np.float64)
    pos = np.arange(P)
    diff = pos[None, :] - pos[:, None]
    mask = np.where(diff >= 0, np.exp(-slope[:, None, None] * np.maximum(diff, 0)), 0.0)
    head = np.arange(D) // HD
    dq = np.exp(-slope[head][:, None] * (pos + 1))
    dk = np.exp(-slope[head][None, :] * (P - 1 - pos)[:, None])
    own = (pos[:, None] // HD == pos[None, :] // HD).astype(np.float64)
    lam = np.exp(-slope * P)[head].reshape(G, P).T[:, :, None] * own[:, None, :]
    f = np.float32
    return {
        "mask": np.ascontiguousarray(mask.transpose(1, 0, 2)).astype(f),
        "dq": np.ascontiguousarray(dq.reshape(G, P, P).transpose(1, 0, 2)).astype(f),
        "dk": dk.astype(f),
        "lam": lam.astype(f),
        "blk": own.astype(f),
        "ident": np.eye(P, dtype=f),
        "rank": np.tile(np.arange(E, 0, -1, dtype=f), (P, 1)),
        "newton": np.tile(np.array([64, -64, -16, -4], f), (P, 1)),
        "keep": np.repeat(np.where(np.arange(NB) % (SEQ // TOK) == 0, 0, -1).astype(np.int32), P).reshape(NB, P, 1),
    }


def kernel(L0_attn_x, L0_attn_w_qkv, L0_attn_b_qkv, L0_attn_w_out, L0_attn_b_out, L0_ffn_router_weight,
           L0_ffn_gate_up_proj, L0_ffn_down_proj, L0_ffn_sh_gate_w, L0_ffn_sh_up_w, L0_ffn_sh_down_w,
           L0_ffn_shared_gate_w):
    import concourse.bacc as bacc
    from concourse.bass_utils import run_bass_kernel_spmd

    A = np.asarray
    x = A(L0_attn_x)
    wT = A(L0_attn_w_qkv).T
    qk = wT[:, :2 * D].reshape(KT, P, 8, P).transpose(2, 1, 0, 3).reshape(8, P, D)
    w_att = np.concatenate([qk, wT[:, 2 * D:].reshape(KT, P, D), A(L0_attn_w_out).T.reshape(KT, P, D)], 0)
    gu = A(L0_ffn_gate_up_proj)
    gate = np.concatenate([A(L0_ffn_sh_gate_w), gu[:, :I_MOE].reshape(E * I_MOE, D)], 0)
    up = np.concatenate([A(L0_ffn_sh_up_w), gu[:, I_MOE:].reshape(E * I_MOE, D)], 0)
    down = np.concatenate([A(L0_ffn_sh_down_w).T, A(L0_ffn_down_proj).transpose(0, 2, 1).reshape(E * I_MOE, D)], 0)

    def stationary(w):
        return w.reshape(NT, P, KT, P).transpose(0, 3, 2, 1).reshape(NT, P, D)
    w_ffn = np.concatenate([stationary(gate), stationary(up), down.reshape(NT, P, D)], 2)
    w_ffn = w_ffn.reshape(NT, P, 2, UNIT).transpose(0, 2, 1, 3)
    rw = np.concatenate([A(L0_ffn_router_weight), A(L0_ffn_shared_gate_w)], 0)
    w_router = np.zeros((P, RWW), rw.dtype)
    w_router[:, :KT * R] = rw.T.reshape(KT, P, R).transpose(1, 0, 2).reshape(P, KT * R)
    b = A(L0_attn_b_qkv)
    t = decay_tables()
    arrays = {
        "x": x.reshape(-1, D), "w_att": w_att, "w_ffn": w_ffn, "w_router": w_router,
        "b_qk": b[:2 * D].reshape(8, P).T, "b_v": b[2 * D:], "b_out": A(L0_attn_b_out),
        "t_mask": t["mask"], "t_dq": t["dq"], "t_dk": t["dk"], "t_lam": t["lam"], "t_blk": t["blk"],
        "t_ident": t["ident"], "t_rank": t["rank"], "t_newton": t["newton"], "t_keep": t["keep"],
    }
    arrays = {n: np.ascontiguousarray(a) for n, a in arrays.items()}
    nc = bacc.Bacc("TRN2", target_bir_lowering=False, num_devices=1)
    args = {n: nc.dram_tensor(n, list(a.shape), mybir.dt.from_np(a.dtype), kind="ExternalInput").ap()
            for n, a in arrays.items()}
    out = nc.dram_tensor("out", [NB * TOK, D], F32, kind="ExternalOutput").ap()
    build(nc, **args, out=out)
    r = run_bass_kernel_spmd(nc, [arrays], core_ids=[0])
    return r.results[0]["out"].reshape(x.shape)
```

```python
import math
from contextlib import ExitStack

import numpy as np

import concourse.bass as bass
from concourse import mybir

ALU = mybir.AluOpType
ACT = mybir.ActivationFunctionType
F32 = mybir.dt.float32
F32R = mybir.dt.float32r
I32 = mybir.dt.int32
AX = mybir.AxisListType

P = 128
D = 512
KT = D // P
HEADS, HD = 16, 32
GH = P // HD
G = HEADS // GH
TOK = 512
NC = TOK // P
NB = 8
SEQ = 1024
E, I_MOE, I_SH = 8, 352, 1408
NT_SH = I_SH // P
NT = NT_SH + E * I_MOE // P
R = E + 1
EPS = 1e-5
LN_STEPS = 10
N1_STEPS = 12
FIN_STEPS = 14
RSQRT_GUESS = float(0x5F3759DF)
UNIT = 768
RAW = 3
WSL = 3
NW = 16
WAS = 4


def c_segments(t):
    if t < NT_SH:
        return [(0, 0, P)]
    out, lo = [], (t - NT_SH) * P
    p = 0
    while p < P:
        e = (lo + p) // I_MOE
        end = min(P, (e + 1) * I_MOE - lo)
        limit = {0: P, 32: 32, 64: 64, 96: 32}[p]
        n = min(end - p, limit)
        out.append((1 + e, p, n))
        p += n
    return out


LAST_TILE = {q: max(t for t in range(NT) if any(s[0] == q for s in c_segments(t))) for q in range(R)}


FIRST_CHUNK = 18
CHUNK_SLOTS = 8


def make_slots():
    s = [[] for _ in range(2 * NT)]

    def put(slot, *piece):
        s[slot].append(piece)

    put(2, "N1A")
    put(3, "N1B")
    for c in range(NC):
        put((3, 4, 7, 8)[c], "N1", c)
        put(6 + c, "T1", c)
        put((4, 5, 8, 9)[c], "W", c)
    for m in range(8):
        put(10 + m, "QK", m)
        put(11 + m, "W", 4 + m)
    for c in range(NC + 1):
        n = FIRST_CHUNK + CHUNK_SLOTS * c
        if c < NC:
            put(n - 1, "Z", c, 0)
            put(n, "KT", c)
            put(n, "Z", c, 1)
            put(n + 1, "S", c, 0)
        if c == 0:
            put(n + 2, "S", c, 1)
            put(n + 2, "V", 0)
            put(n + 2, "Z", c, 2)
            put(n + 3, "V", 1)
            put(n + 3, "Z", c, 3)
            put(n + 3, "IP", c, 0)
            put(n + 4, "S", c, 2)
            put(n + 4, "V", 2)
            put(n + 5, "V", 3)
            put(n + 5, "S", c, 3)
            put(n + 5, "W", 12)
            put(n + 6, "IP", c, 1)
            put(n + 6, "W", 13)
            put(n + 7, "ST", c)
            put(n + 7, "W", 14)
            put(n + 8, "W", 15)
        elif c < NC:
            if c > 1:
                put(n + 1, "OUT", c - 1)
            put(n + 2, "S", c, 1)
            if c == 1:
                put(n + 2, "OUT", 0)
            put(n + 2, "Z", c, 2)
            put(n + 3, "Z", c, 3)
            put(n + 3, "IP", c, 0)
            put(n + 3, "LO", c - 1)
            put(n + 4, "S", c, 2)
            put(n + 5, "S", c, 3)
            put(n + 5, "L", c - 1)
            put(n + 6, "IP", c, 1)
            put(n + 7, "ST", c)
            put(n + 7, "T2", c - 1)
    put(n, "OUT", NC - 1)
    put(n + 1, "LO", NC - 1)
    put(n + 3, "L", NC - 1)
    put(n + 5, "T2", NC - 1)
    put(n + 6, "R1")
    put(n + 7, "R2")
    put(n + 7, "SM1")
    put(n + 9, "SM2")
    put(n + 9, "SM3")
    put(n + 11, "SM4")
    put(n + 12, "R3")
    return s


SLOTS = make_slots()
PIECES = [p for slot in SLOTS for p in slot]
PARTS = {"N1A": "V", "N1B": "V", "N1": "V", "W": "AV", "T1": "PAV", "QK": "PA", "V": "PV", "KT": "PV", "Z": "A", "S": "PV",
         "IP": "PAV", "ST": "PV", "OUT": "PV", "LO": "V", "L": "V", "T2": "PAV", "R1": "PA", "R2": "PV",
         "SM1": "AV", "SM2": "V", "SM3": "V", "SM4": "V", "R3": "PA"}
ORDER = {e: [p for p in PIECES if e in PARTS[p[0]]] for e in "PAV"}
STEPS = {"N1B": N1_STEPS, "LO": LN_STEPS, "L": LN_STEPS + 1, "ST": 1, "SM1": 1, "SM2": 7, "SM3": 5, "SM4": 7}
STEP_BASE, _n = {}, 0
for _p in PIECES:
    STEP_BASE[_p] = _n
    _n += STEPS.get(_p[0], 0)
STEPS_PER_BLOCK = _n


def done(engine, a, *piece):
    return a * len(ORDER[engine]) + ORDER[engine].index(piece) + 1


def build(nc, x, w_att, w_ffn, w_router, b_qk, b_v, b_out, t_mask, t_dq, t_dk, t_lam, t_blk, t_ident, t_rank, t_newton,
          t_keep, out):
    x_d = x.rearrange("(b c p) d -> b c p d", b=NB, c=NC)
    out_d = out.rearrange("(b c p) d -> b c p d", b=NB, c=NC)
    x1_d = nc.dram_tensor("x1_scratch", [NB, NC, P, D], F32, kind="Internal").ap()
    rows_d = nc.dram_tensor("router_scratch", [NB, R, TOK], F32, kind="Internal").ap()

    with ExitStack() as ctx:
        def sb(name, shape, dt=F32):
            return ctx.enter_context(nc.sbuf_tensor(name, [P] + shape, dt))

        def sem(name):
            return ctx.enter_context(nc.semaphore(name))

        mask = sb("decay_mask", [HEADS, P])
        dq = sb("decay_q", [G, P])
        dk = sb("decay_k", [D])
        lam = sb("state_decay", [G])
        blk = sb("own_block", [P])
        ident = sb("identity", [P])
        newton = sb("newton", [4])
        rank = sb("rank", [E])
        keep = sb("keep_state", [1], I32)
        bqk = sb("bias_qk", [8])
        bv = sb("bias_v", [D])
        bo = sb("bias_out", [D])
        rw_hi = sb("router_hi", [RWW], F32R)
        rw_lo = sb("router_lo", [RWW], F32R)

        wa_raw = sb("att_w_raw", [2, D])
        wa_hi = sb("att_w_hi", [WAS, D], F32R)
        wa_lo = sb("att_w_lo", [WAS, D], F32R)
        xin = sb("x_in", [NC, D])
        nst = sb("x_stats", [NC, 6])
        nmv = sb("x_mean_var", [NC, 2])
        nvs = sb("x_var_scaled", [4, NC])
        nrstd, nrtmp = sb("x_rstd", [NC]), sb("x_rstd_tmp", [NC])
        xn = sb("x_normed", [D])
        xs_hi = sb("xT_staged_hi", [KT, TOK], F32R)
        xs_lo = sb("xT_staged_lo", [KT, TOK], F32R)
        qT = sb("qT", [G, TOK])
        kT = sb("kT", [G, TOK])
        v = sb("v", [NC, D])
        qz = sb("q_one_head", [2, GH, P])
        qd = sb("q_decayed", [G, P])
        kd = sb("k_decayed", [D])
        probs = sb("probsT", [2, GH, P])
        state = sb("state", [G, P])
        state_new = sb("state_new", [G, P])
        oT_hi = sb("attT_hi", [G, P], F32R)
        oT_lo = sb("attT_lo", [G, P], F32R)
        o = sb("projected", [D])
        rw_raw = v[:, 0, 0:RWW]
        x1 = sb("x1", [2, D])
        st = sb("stats", [6])
        mv = sb("mean_var", [2])
        vs4, rstd, rtmp = sb("var_scaled", [4, 1]), sb("rstd", [1]), sb("rstd_tmp", [1])

        lgT = sb("logitsT", [TOK])
        lg = sb("logits", [NC, R])
        sm = {n: sb("router_" + n, [NC, w]) for n, w in [
            ("max", 1), ("d", E), ("e", E), ("z", 1), ("sum", 1), ("rcp", 1), ("p", E), ("m1", 1), ("m2", 1),
            ("oh", E), ("key", E), ("km", 1), ("oh1", E), ("oh2", E), ("s", 1), ("rs", 1), ("a", E), ("b", E)]}
        comb = sb("combine", [NC, R])

        xt_hi = sb("xT_hi", [KT, TOK], F32R)
        xt_lo = sb("xT_lo", [KT, TOK], F32R)
        raw = sb("ffn_w_raw", [RAW, UNIT])
        w_hi = sb("ffn_w_hi", [WSL, 3 * D], F32R)
        w_lo = sb("ffn_w_lo", [WSL, 3 * D], F32R)
        crow = sb("router_rows", [3, TOK])
        sg = sb("silu_gate", [TOK])
        hid = sb("hidden", [TOK])
        h_hi = sb("hidden_hi", [2, TOK], F32R)
        h_lo = sb("hidden_lo", [2, TOK], F32R)
        x1r = sb("x1_reload", [NC, D])
        fst = sb("fin_stats", [NC, 6])
        fmv = sb("fin_mean_var", [NC, 2])
        fvs = sb("fin_var_scaled", [4, NC])
        frstd, frtmp, fshift = sb("fin_rstd", [NC]), sb("fin_rstd_tmp", [NC]), sb("fin_shift", [NC])

        acc = ctx.enter_context(nc.psum_tensor("ffn_acc", [P, NC, D], F32))
        gate_ps = ctx.enter_context(nc.psum_tensor("gate", [P, TOK], F32))
        up_ps = ctx.enter_context(nc.psum_tensor("up", [P, TOK], F32))
        bank = ctx.enter_context(nc.psum_tensor("piece_banks", [P, 2, D], F32))

        const_in = sem("const_in")
        late_in = sem("late_const_in")
        const_v = sem("const_v")
        const_a = sem("const_a")
        p_piece, a_piece, v_piece = sem("pe_piece"), sem("act_piece"), sem("dve_piece")
        v_step = sem("dve_step")
        passed = sem("wait_passed")
        a_exp = sem("exp_done")
        x0_in = sem("first_x_in")
        x_in = [sem(f"x_in{i}") for i in range(NC)]
        wa_in = [sem(f"att_w_in{i}") for i in range(2)]
        keep_in = sem("keep_in")
        x1_out = [sem(f"x1_out{i}") for i in range(2)]
        rows_out = sem("rows_out")
        row_in = [sem(f"row_in{i}") for i in range(3)]
        raw_in = [sem(f"raw_in{i}") for i in range(RAW)]
        whi_done, wlo_done = sem("whi_done"), sem("wlo_done")
        xt_hi_done, xt_lo_done = sem("xt_hi_done"), sem("xt_lo_done")
        gate_done, up_done, down_done = sem("gate_done"), sem("up_done"), sem("down_done")
        silu_done, gated_done, hid_done = sem("silu_done"), sem("gated_done"), sem("hid_done")
        hhi_done, hlo_done = sem("hhi_done"), sem("hlo_done")
        acc_done = sem("acc_chunk_done")
        fin_step = sem("fin_step")
        fin_shift = sem("fin_shift_done")
        out_done = sem("out_done")
        x1r_in = [sem(f"x1r_in{i}") for i in range(NC)]
        out_stored = [sem(f"out_stored{i}") for i in range(NC)]

        def wait(eng, s, value):
            if isinstance(value, int) and value <= 0:
                return
            eng.wait_ge(s, value)

        def bank_of(piece):
            return ORDER["P"].index(piece) % 2

        N_CONST, N_LATE = 3, 9

        def is_first(a):
            return isinstance(a, int) and a == 0

        def settle(eng, a):
            if not isinstance(a, int):
                eng.sem_inc(passed, 1)

        def sp_att_weights(sp, a, u):
            if u >= 2:
                sp.wait_ge(v_piece, done("V", a, "W", u - 2))
            elif not is_first(a):
                sp.wait_ge(v_piece, done("V", a - 1, "W", NW - 2 + u))
            sp.dma_start(out=wa_raw[:, u % 2, :], in_=w_att[u]).then_inc(wa_in[u % 2], 16)

        def sp_slot(sp, a, s):
            if s == 0:
                sp_att_weights(sp, a, 0)
                sp_att_weights(sp, a, 1)
            for piece in SLOTS[s]:
                if piece[0] == "W" and piece[1] + 2 < NW:
                    sp_att_weights(sp, a, piece[1] + 2)

        def sp_raw(sp, f, t, half):
            if t >= NT:
                f, t = f + 1, t - NT
            n = 2 * t + half
            wait(sp, wlo_done, f * 2 * NT + n - RAW + 1)
            sp.dma_start(out=raw[:, n % RAW, :], in_=w_ffn[t, half]).then_inc(raw_in[n % RAW], 16)

        AHEAD = 1

        def sp_body(sp, f, last):
            for t in range(NT):
                if not (last and t + AHEAD + 1 >= NT):
                    for half in range(2):
                        sp_raw(sp, f, t + AHEAD + 1, half)
                if not last:
                    sp_slot(sp, f + 1, 2 * t)
                    sp_slot(sp, f + 1, 2 * t + 1)

        def pool_x(pool, a, c):
            pool.wait_ge(v_piece, done("V", a - 1, "L", c))
            settle(pool, a)
            pool.dma_start(out=xin[:, c, :], in_=x_d[a, c]).then_inc(x_in[c], 16)

        def pool_slot(pool, a, s):
            if s == 0:
                for c in range(0 if is_first(a) else NC):
                    pool_x(pool, a, c)
                if not is_first(a):
                    pool.wait_ge(v_piece, done("V", a - 1, "KT", 0))
                settle(pool, a)
                pool.dma_start(out=keep[:, :], in_=t_keep[a]).then_inc(keep_in, 16)
            for piece in SLOTS[s]:
                kind = piece[0]
                if kind == "L":
                    c = piece[1]
                    pool.wait_ge(v_piece, done("V", a, "L", c))
                    settle(pool, a)
                    pool.dma_start(out=x1_d[a, c], in_=x1[:, c % 2, :]).then_inc(x1_out[c % 2], 16)
                if kind == "R3":
                    pool.wait_ge(a_piece, done("A", a, "R3"))
                    settle(pool, a)
                    pool.dma_start(out=rows_d[a], in_=lgT[0:R, :]).then_inc(rows_out, 16)

        def pool_row(pool, f, q):
            pool.wait_ge(rows_out, 16 * (f + 1))
            if q >= 3:
                pool.wait_ge(hid_done, NT * f + LAST_TILE[q - 3] + 1)
            else:
                wait(pool, hid_done, NT * (f - 1) + LAST_TILE[q + R - 3] + 1)
            settle(pool, f)
            row = E if q == 0 else q - 1
            pool.dma_start(out=crow[:, q % 3, :], in_=rows_d[f, row].partition_broadcast(P)).then_inc(row_in[q % 3], 16)

        def pool_stores(pool, f):
            for c in range(NC):
                pool.wait_ge(out_done, NC * f + c + 1)
                settle(pool, f)
                pool.dma_start(out=out_d[f, c], in_=x1r[:, c, :]).then_inc(out_stored[c], 16)

        def pool_body(pool, f, first, last):
            for t in range(NT):
                if not last:
                    pool_slot(pool, f + 1, 2 * t)
                if t == 0 and not first:
                    pool_stores(pool, f - 1)
                if not last:
                    pool_slot(pool, f + 1, 2 * t + 1)
                for q in range(3, R):
                    if LAST_TILE[q - 3] == t:
                        pool_row(pool, f, q)
                if t == NT - 4:
                    for c in range(NC):
                        x1_reload(pool, f, c)
            if not last:
                for q in range(3):
                    pool_row(pool, f + 1, q)
            else:
                pool_stores(pool, f)

        def x1_reload(pool, f, c):
            pool.wait_ge(x1_out[c % 2], 16 * (NC // 2) * (f + 1))
            wait(pool, out_stored[c], 16 * f)
            settle(pool, f)
            pool.dma_start(out=x1r[:, c, :], in_=x1_d[f, c]).then_inc(x1r_in[c], 16)

        def three(pe, out_ap, l_hi, l_lo, r_hi, r_lo, start, stop):
            pe.matmul(out_ap, l_hi, r_hi, start=start, stop=False)
            pe.matmul(out_ap, l_hi, r_lo, start=False, stop=False)
            return pe.matmul(out_ap, l_lo, r_hi, start=False, stop=stop)

        def pe_piece(pe, a, piece):
            kind = piece[0]
            b = bank[:, bank_of(piece), :]
            i = ORDER["P"].index(piece)
            if i >= 2:
                old = ORDER["P"][i - 2]
                if "A" in PARTS[old[0]]:
                    pe.wait_ge(a_piece, done("A", a, *old))
                if "V" in PARTS[old[0]]:
                    pe.wait_ge(v_piece, done("V", a, *old))
            else:
                wait(pe, a_piece, a * len(ORDER["A"]))
                wait(pe, v_piece, a * len(ORDER["V"]))
            if kind in ("T1", "T2"):
                c = piece[1]
                pe.wait_ge(v_piece, done("V", a, "N1" if kind == "T1" else "L", c))
                normed = o if kind == "T1" and c % 2 else xn
                for k in range(KT):
                    mm = pe.transpose(b[:, k * P:(k + 1) * P], normed[:, k * P:(k + 1) * P], ident[:, :])
            elif kind == "QK":
                m = piece[1]
                pe.wait_ge(a_piece, done("A", a, "W", m))
                pe.wait_ge(v_piece, done("V", a, "W", m))
                if m == 0:
                    pe.wait_ge(v_piece, done("V", a, "T1", NC - 1))
                for k in range(KT):
                    ks = slice(k * P, (k + 1) * P)
                    mm = three(pe, b, wa_hi[:, m % WAS, ks], wa_lo[:, m % WAS, ks], xs_hi[:, k, :], xs_lo[:, k, :],
                               k == 0, k == KT - 1)
            elif kind == "V":
                c = piece[1]
                cs = slice(c * P, (c + 1) * P)
                if c == 0:
                    pe.wait_ge(a_piece, done("A", a, "W", 11))
                    pe.wait_ge(v_piece, done("V", a, "W", 11))
                for k in range(KT):
                    mm = three(pe, b, xs_hi[:, k, cs], xs_lo[:, k, cs], wa_hi[:, k, :], wa_lo[:, k, :],
                               k == 0, k == KT - 1)
            elif kind == "KT":
                c = piece[1]
                if c == 0:
                    pe.wait_ge(a_piece, done("A", a, "QK", 7))
                for g in range(G):
                    mm = pe.transpose(b[:, g * P:(g + 1) * P], kT[:, g, c * P:(c + 1) * P], ident[:, :])
            elif kind == "S":
                c, g = piece[1:]
                pe.wait_ge(a_piece, done("A", a, "Z", c, g))
                mm = pe.matmul(b, kT[:, g, c * P:(c + 1) * P], qz[:, g % 2].rearrange("p h t -> p (h t)"),
                               start=True, stop=True)
            elif kind == "IP":
                c, half = piece[1:]
                pe.wait_ge(v_piece, done("V", a, "S", c, 2 * half + 1))
                for gl in range(2):
                    g = 2 * half + gl
                    cols = slice(gl * P, (gl + 1) * P)
                    pe.matmul(b[:, cols], state[:, g, :], qd[:, g, :], start=(gl == 0), stop=False,
                              skip_group_check=True)
                    for j in range(GH):
                        r = slice(j * HD, (j + 1) * HD)
                        mm = pe.matmul(b[r, cols], v[:, c, g * P + j * HD:g * P + (j + 1) * HD],
                                       probs[:, g % 2, j, :], start=False, stop=(gl == 1), skip_group_check=True)
            elif kind == "ST":
                c = piece[1]
                for g in range(G):
                    gs = slice(g * P, (g + 1) * P)
                    mm = pe.matmul(b[:, gs], kd[:, gs], v[:, c, gs], start=True, stop=True)
            elif kind == "OUT":
                c = piece[1]
                if c == 0:
                    pe.wait_ge(a_piece, done("A", a, "W", 15))
                    pe.wait_ge(v_piece, done("V", a, "W", 15))
                pe.wait_ge(v_piece, done("V", a, "IP", c, 1))
                for k in range(KT):
                    mm = three(pe, b, oT_hi[:, k, :], oT_lo[:, k, :], wa_hi[:, k, :], wa_lo[:, k, :],
                               k == 0, k == KT - 1)
            elif kind == "R1":
                pe.wait_ge(v_piece, done("V", a, "T2", NC - 1))
                for k in range(KT):
                    ks = slice(k * R, k * R + P)
                    mm = three(pe, b, rw_hi[:, ks], rw_lo[:, ks], xs_hi[:, k, :], xs_lo[:, k, :],
                               k == 0, k == KT - 1)
            elif kind == "R2":
                pe.wait_ge(a_piece, done("A", a, "R1"))
                for c in range(NC):
                    mm = pe.matmul(b[:, c * R:(c + 1) * R], lgT[0:R, c * P:(c + 1) * P], ident[0:R, 0:R],
                                   start=True, stop=True)
            elif kind == "R3":
                pe.wait_ge(v_piece, done("V", a, "SM4"))
                for c in range(NC):
                    mm = pe.matmul(b[0:R, c * P:(c + 1) * P], comb[:, c, :], ident[:, :], start=True, stop=True)
            mm.then_inc(p_piece, 1)

        def pe_slot(pe, a, s):
            for piece in SLOTS[s]:
                if "P" in PARTS[piece[0]]:
                    pe_piece(pe, a, piece)

        def pe_gate_up(pe, f, t):
            n = NT * f + t
            pe.wait_ge(whi_done, 2 * (n + 1))
            pe.wait_ge(wlo_done, 2 * (n + 1))
            if t == 0:
                pe.wait_ge(xt_hi_done, f + 1)
                pe.wait_ge(xt_lo_done, f + 1)
            wait(pe, silu_done, n)
            for part, dst, signal in ((0, gate_ps, gate_done), (1, up_ps, up_done)):
                if part:
                    wait(pe, gated_done, n)
                for k in range(KT):
                    ks = slice(part * D + k * P, part * D + (k + 1) * P)
                    mm = three(pe, dst[:, :], w_hi[:, t % WSL, ks], w_lo[:, t % WSL, ks], xt_hi[:, k, :],
                               xt_lo[:, k, :], k == 0, k == KT - 1)
                mm.then_inc(signal, 1)

        def pe_down(pe, f, t):
            n = NT * f + t
            pe.wait_ge(hhi_done, n + 1)
            pe.wait_ge(hlo_done, n + 1)
            down = slice(2 * D, 3 * D)
            for c in range(NC):
                cs = slice(c * P, (c + 1) * P)
                if t == 0 and c == 0:
                    wait(pe, out_done, NC * f)
                mm = three(pe, acc[:, c, :], h_hi[:, t % 2, cs], h_lo[:, t % 2, cs], w_hi[:, t % WSL, down],
                           w_lo[:, t % WSL, down], t == 0, t == NT - 1)
                if t == NT - 1 and c < NC - 1:
                    mm.then_inc(acc_done, 1)
            mm.then_inc(down_done, 1)

        def pe_body(pe, f, last):
            for t in range(NT):
                if t:
                    pe_gate_up(pe, f, t)
                if not last:
                    pe_slot(pe, f + 1, 2 * t)
                if t:
                    pe_down(pe, f, t - 1)
                if not last:
                    pe_slot(pe, f + 1, 2 * t + 1)
            pe_down(pe, f, NT - 1)
            if not last:
                pe_gate_up(pe, f + 1, 0)

        def chunked(b):
            return b.rearrange("p (k t) -> p k t", t=P)

        def act_piece(act, a, piece):
            kind = piece[0]
            if "P" in PARTS[kind]:
                b = bank[:, bank_of(piece), :]
                act.wait_ge(p_piece, done("P", a, *piece))
            if kind in ("T1", "T2"):
                c = piece[1]
                op = act.copy(xs_hi[:, :, c * P:(c + 1) * P], chunked(b))
            elif kind == "W":
                u = piece[1]
                act.wait_ge(wa_in[u % 2], 16 * (a * (NW // 2) + u // 2 + 1))
                if u >= 12:
                    act.wait_ge(p_piece, done("P", a, "V", NC - 1))
                elif u >= WAS:
                    act.wait_ge(p_piece, done("P", a, "QK", u - WAS))
                else:
                    wait(act, p_piece, a * len(ORDER["P"]))
                op = act.copy(wa_hi[:, u % WAS, :], wa_raw[:, u % 2, :])
            elif kind == "QK":
                m = piece[1]
                dst = qT if m < G else kT
                op = act.activation(dst[:, m % G, :], b, ACT.Identity, bias=bqk[:, m:m + 1])
            elif kind == "Z":
                c, g = piece[1:]
                if (c, g) == (0, 0):
                    act.wait_ge(a_piece, done("A", a, "QK", G - 1))
                if 4 * c + g >= 2:
                    cc, gg = divmod(4 * c + g - 2, G)
                    act.wait_ge(p_piece, done("P", a, "S", cc, gg))
                for j in range(GH):
                    r = slice(j * HD, (j + 1) * HD)
                    op = act.copy(qz[r, g % 2, j, :], qT[r, g, c * P:(c + 1) * P])
            elif kind == "IP":
                c, half = piece[1:]
                if half == 0 and c > 0:
                    act.wait_ge(p_piece, done("P", a, "OUT", c - 1))
                op = act.copy(oT_hi[:, 2 * half:2 * half + 2, :], chunked(b[:, 0:2 * P]))
            elif kind == "R1":
                wait(act, rows_out, 16 * a)
                op = act.copy(lgT[0:R, :], b[0:R, :])
            elif kind == "SM1":
                act.wait_ge(v_piece, done("V", a, "SM1"))
                act.activation(sm["z"][:, :, :], lg[:, :, E:R], ACT.Exp, scale=-1.0)
                op = act.activation(sm["e"][:, :, :], sm["d"][:, :, :], ACT.Exp)
            elif kind == "R3":
                op = act.copy(lgT[0:R, :], b[0:R, :])
            op.then_inc(a_piece, 1)

        def act_slot(act, a, s):
            for piece in SLOTS[s]:
                if "A" in PARTS[piece[0]]:
                    act_piece(act, a, piece)

        def split_wait(eng, f, t, half):
            n = 2 * t + half
            eng.wait_ge(raw_in[n % RAW], 16 * (f * (2 * NT // RAW) + n // RAW + 1))
            if half == 0:
                wait(eng, down_done, NT * f + t - WSL + 1)

        def act_split(act, f, t):
            if t >= NT:
                f, t = f + 1, t - NT
            for half in range(2):
                split_wait(act, f, t, half)
                us = slice(half * UNIT, (half + 1) * UNIT)
                act.copy(w_hi[:, t % WSL, us], raw[:, (2 * t + half) % RAW, :]).then_inc(whi_done, 1)

        def act_xt(act, f):
            wait(act, up_done, NT * f)
            act.wait_ge(a_piece, done("A", f, "T2", NC - 1))
            act.copy(xt_hi[:, :, :], xs_hi[:, :, :].bitcast(F32)).then_inc(xt_hi_done, 1)

        def act_fin(act, f):
            act.wait_ge(fin_step, FIN_STEPS * (f + 1))
            for c in range(NC):
                act.wait_ge(x1r_in[c], 16 * (f + 1))
                act.activation(x1r[:, c, :], x1r[:, c, :], ACT.Identity,
                               bias=fshift[:, c:c + 1]).then_inc(fin_shift, 1)

        def act_silu(act, f, t):
            n = NT * f + t
            act.wait_ge(gate_done, n + 1)
            wait(act, gated_done, n)
            act.activation(sg[:, :], gate_ps[:, :], ACT.Silu).then_inc(silu_done, 1)

        def act_body(act, f, last):
            for t in range(NT):
                n = NT * f + t
                if t and t + AHEAD < NT or t == NT - 1 and not last:
                    act_split(act, f, t + AHEAD)
                if t:
                    act_silu(act, f, t)
                act.wait_ge(hid_done, n + 1)
                wait(act, down_done, NT * f + t - 1 if t >= 2 else NT * f)
                act.copy(h_hi[:, t % 2, :], hid[:, :]).then_inc(hhi_done, 1)
                if not last:
                    act_slot(act, f + 1, 2 * t)
                    act_slot(act, f + 1, 2 * t + 1)
            if not last:
                act_xt(act, f + 1)
                act_split(act, f + 1, 1)
                act_silu(act, f + 1, 0)
            act_fin(act, f)

        def rsqrt(ve, var, n, vs, y, t, chain):
            chain(ve.scalar_tensor_tensor(out=vs[:, :, :], in0=var.unsqueeze(1).to_broadcast([P, 4, n]), scalar=EPS,
                                          in1=newton[:, :].unsqueeze(2).to_broadcast([P, 4, n]), op0=ALU.add,
                                          op1=ALU.mult))
            chain(ve.tensor_scalar(y[:, :].bitcast(I32), vs[:, 0, :].bitcast(I32), -0.5, RSQRT_GUESS, ALU.mult,
                                   ALU.add))
            for i in range(3):
                if n == 1:
                    chain(ve.scalar_tensor_tensor(out=t[:, :], in0=y[:, :], scalar=vs[:, i + 1, 0:1], in1=y[:, :],
                                                  op0=ALU.mult, op1=ALU.mult))
                else:
                    chain(ve.tensor_tensor(t[:, :], y[:, :], y[:, :], ALU.mult))
                    chain(ve.tensor_tensor(t[:, :], t[:, :], vs[:, i + 1, :], ALU.mult))
                chain(ve.scalar_tensor_tensor(out=y[:, :], in0=t[:, :], scalar=3.0, in1=y[:, :], op0=ALU.add,
                                              op1=ALU.mult))

        def chained(eng, sem_, base):
            count = [0]

            def chain(op):
                count[0] += 1
                op.then_inc(sem_, 1)
                eng.wait_ge(sem_, base + count[0])
            return chain

        def layernorm(ve, src, dst, a, piece, n0):
            chain = chained(ve, v_step, a * STEPS_PER_BLOCK + STEP_BASE[piece] + n0)
            chain(ve.bn_stats(st[:, :], src))
            settle(ve, a)
            chain(ve.bn_aggr(mv[:, :], st[:, :]))
            rsqrt(ve, mv[:, 1:2], 1, vs4, rstd, rtmp, chain)
            return ve.tensor_scalar(dst, src, mv[:, 0:1], rstd[:, 0:1], ALU.subtract, ALU.mult)

        def dve_piece(ve, a, piece):
            kind = piece[0]
            if "P" in PARTS[kind]:
                b = bank[:, bank_of(piece), :]
                ve.wait_ge(p_piece, done("P", a, *piece))

            def step(op, n):
                op.then_inc(v_step, 1)
                ve.wait_ge(v_step, a * STEPS_PER_BLOCK + STEP_BASE[piece] + n)

            if kind == "N1A":
                wait(ve, v_piece, a * len(ORDER["V"]))
                if is_first(a):
                    ve.wait_ge(x0_in, 16 * NC)
                for c in range(NC):
                    if not is_first(a):
                        ve.wait_ge(x_in[c], 16 * a)
                    op = ve.bn_stats(nst[:, c, :], xin[:, c, :])
            elif kind == "N1B":
                chain = chained(ve, v_step, a * STEPS_PER_BLOCK + STEP_BASE[piece])
                ve.wait_ge(v_piece, done("V", a, "N1A"))
                settle(ve, a)
                for c in range(NC):
                    op = ve.bn_aggr(nmv[:, c, :], nst[:, c, :])
                chain(op)
                rsqrt(ve, nmv[:, :, 1], NC, nvs, nrstd, nrtmp, chain)
                ve.sem_inc(v_piece, 1)
                return
            elif kind == "N1":
                c = piece[1]
                if c >= 2:
                    ve.wait_ge(p_piece, done("P", a, "T1", c - 2))
                op = ve.tensor_scalar((xn, o)[c % 2][:, :], xin[:, c, :], nmv[:, c, 0:1], nrstd[:, c:c + 1], ALU.subtract,
                                      ALU.mult)
            elif kind in ("T1", "T2"):
                c = piece[1]
                cs = slice(c * P, (c + 1) * P)
                ve.wait_ge(a_piece, done("A", a, *piece))
                op = ve.tensor_tensor(xs_lo[:, :, cs], chunked(b), xs_hi[:, :, cs].bitcast(F32), ALU.subtract)
            elif kind == "W":
                u = piece[1]
                ve.wait_ge(a_piece, done("A", a, *piece))
                op = ve.tensor_tensor(wa_lo[:, u % WAS, :], wa_raw[:, u % 2, :], wa_hi[:, u % WAS, :].bitcast(F32),
                                      ALU.subtract)
            elif kind == "V":
                op = ve.tensor_tensor(v[:, piece[1], :], b, bv[:, :], ALU.add)
            elif kind == "KT":
                c = piece[1]
                if c == 0:
                    ve.wait_ge(keep_in, 16 * (a + 1))
                    wait(ve, v_piece, (a - 1) * len(ORDER["V"]) + ORDER["V"].index(("ST", NC - 1)) + 1
                         if not isinstance(a, int) or a > 0 else 0)
                    s_flat = state[:, :, :].rearrange("p g d -> p (g d)").bitcast(I32)
                    ve.tensor_tensor(s_flat, s_flat, keep[:, :].to_broadcast([P, D]), ALU.bitwise_and)
                    ve.wait_ge(a_piece, done("A", a, "QK", G - 1))
                ve.tensor_tensor(qd[:, :, :], qT[:, :, c * P:(c + 1) * P], dq[:, :, :], ALU.mult)
                op = ve.tensor_tensor(kd[:, :], b, dk[:, :], ALU.mult)
            elif kind == "S":
                c, g = piece[1:]
                op = ve.tensor_tensor(probs[:, g % 2, :, :], chunked(b), mask[:, GH * g:GH * (g + 1), :], ALU.mult)
            elif kind == "IP":
                c, half = piece[1:]
                gs = slice(2 * half, 2 * half + 2)
                ve.wait_ge(a_piece, done("A", a, *piece))
                op = ve.tensor_tensor(oT_lo[:, gs, :], chunked(b[:, 0:2 * P]), oT_hi[:, gs, :].bitcast(F32),
                                      ALU.subtract)
            elif kind == "ST":
                ve.tensor_tensor(state_new[:, :, :], chunked(b), blk[:, :].unsqueeze(1).to_broadcast([P, G, P]),
                                 ALU.mult).then_inc(v_step, 1)
                ve.wait_ge(v_step, a * STEPS_PER_BLOCK + STEP_BASE[piece] + 1)
                for g in range(G):
                    op = ve.scalar_tensor_tensor(out=state[:, g, :], in0=state[:, g, :], scalar=lam[:, g:g + 1],
                                                 in1=state_new[:, g, :], op0=ALU.mult, op1=ALU.add)
            elif kind == "OUT":
                op = ve.tensor_tensor(o[:, :], b, bo[:, :], ALU.add)
            elif kind == "LO":
                ve.wait_ge(v_piece, done("V", a, "OUT", piece[1]))
                op = layernorm(ve, o[:, :], o[:, :], a, piece, 0)
            elif kind == "L":
                c = piece[1]
                n = a * (NC // 2) + c // 2
                wait(ve, x1_out[c % 2], 16 * n)
                ve.wait_ge(v_piece, done("V", a, "LO", c))
                step(ve.tensor_tensor(x1[:, c % 2, :], o[:, :], xin[:, c, :], ALU.add), 1)
                if c:
                    ve.wait_ge(p_piece, done("P", a, "T2", c - 1))
                op = layernorm(ve, x1[:, c % 2, :], xn[:, :], a, piece, 1)
            elif kind == "R2":
                op = ve.tensor_copy(lg[:, :, :], b[:, 0:NC * R].rearrange("p (c r) -> p c r", r=R))
            elif kind == "SM1":
                ve.wait_ge(v_piece, done("V", a, "R2"))
                l8 = lg[:, :, 0:E]
                step(ve.tensor_reduce(sm["max"][:, :, :], l8, AX.X, ALU.max), 1)
                op = ve.tensor_tensor(sm["d"][:, :, :], l8, wide(sm["max"]), ALU.subtract)
            elif kind == "SM2":
                ve.wait_ge(a_piece, done("A", a, "SM1"))
                step(ve.tensor_reduce(sm["sum"][:, :, :], sm["e"][:, :, :], AX.X, ALU.add), 1)
                step(ve.reciprocal(sm["rcp"][:, :, :], sm["sum"][:, :, :]), 2)
                step(ve.tensor_tensor(sm["p"][:, :, :], sm["e"][:, :, :], wide(sm["rcp"]), ALU.mult), 3)
                op = first_of_largest(ve, step, 3, "p", "m1", "oh1")
            elif kind == "SM3":
                ve.wait_ge(v_piece, done("V", a, "SM2"))
                step(ve.scalar_tensor_tensor(out=sm["d"][:, :, :], in0=sm["oh1"][:, :, :], scalar=-4.0,
                                             in1=sm["p"][:, :, :], op0=ALU.mult, op1=ALU.add), 1)
                op = first_of_largest(ve, step, 1, "d", "m2", "oh2")
            elif kind == "SM4":
                ve.wait_ge(v_piece, done("V", a, "SM3"))
                step(ve.tensor_tensor(sm["s"][:, :, :], sm["m1"][:, :, :], sm["m2"][:, :, :], ALU.add), 1)
                step(ve.reciprocal(sm["rs"][:, :, :], sm["s"][:, :, :]), 2)
                step(ve.tensor_tensor(sm["a"][:, :, :], sm["oh1"][:, :, :], wide(sm["m1"]), ALU.mult), 3)
                step(ve.tensor_tensor(sm["b"][:, :, :], sm["oh2"][:, :, :], wide(sm["m2"]), ALU.mult), 4)
                step(ve.tensor_tensor(sm["a"][:, :, :], sm["a"][:, :, :], sm["b"][:, :, :], ALU.add), 5)
                step(ve.tensor_tensor(comb[:, :, 0:E], sm["a"][:, :, :], wide(sm["rs"]), ALU.mult), 6)
                step(ve.tensor_scalar(sm["s"][:, :, :], sm["z"][:, :, :], 1.0, None, ALU.add), 7)
                op = ve.reciprocal(comb[:, :, E:R], sm["s"][:, :, :])
            op.then_inc(v_piece, 1)

        def wide(t):
            return t[:, :, :].to_broadcast([P, NC, E])

        def first_of_largest(ve, step, n, src, largest, onehot):
            step(ve.tensor_reduce(sm[largest][:, :, :], sm[src][:, :, :], AX.X, ALU.max), n + 1)
            step(ve.tensor_tensor(sm["oh"][:, :, :], sm[src][:, :, :], wide(sm[largest]), ALU.is_equal), n + 2)
            step(ve.tensor_tensor(sm["key"][:, :, :], sm["oh"][:, :, :],
                                  rank[:, :].unsqueeze(1).to_broadcast([P, NC, E]), ALU.mult), n + 3)
            step(ve.tensor_reduce(sm["km"][:, :, :], sm["key"][:, :, :], AX.X, ALU.max), n + 4)
            return ve.tensor_tensor(sm[onehot][:, :, :], sm["key"][:, :, :], wide(sm["km"]), ALU.is_equal)

        def dve_slot(ve, a, s):
            for piece in SLOTS[s]:
                if "V" in PARTS[piece[0]]:
                    dve_piece(ve, a, piece)

        def dve_split(ve, f, t):
            if t >= NT:
                f, t = f + 1, t - NT
            for half in range(2):
                us = slice(half * UNIT, (half + 1) * UNIT)
                ve.wait_ge(whi_done, f * 2 * NT + 2 * t + half + 1)
                ve.tensor_tensor(w_lo[:, t % WSL, us], raw[:, (2 * t + half) % RAW, :],
                                 w_hi[:, t % WSL, us].bitcast(F32), ALU.subtract).then_inc(wlo_done, 1)

        def dve_xt(ve, f):
            wait(ve, up_done, NT * f)
            ve.wait_ge(v_piece, done("V", f, "T2", NC - 1))
            ve.tensor_copy(xt_lo[:, :, :], xs_lo[:, :, :].bitcast(F32)).then_inc(xt_lo_done, 1)

        def dve_fin_stats(ve, f, last):
            for c in range(NC):
                if c < NC - 1:
                    ve.wait_ge(acc_done, (NC - 1) * f + c + 1)
                else:
                    ve.wait_ge(down_done, NT * (f + 1))
                op = ve.bn_stats(fst[:, c, :], acc[:, c, :])
            op.then_inc(fin_step, 1)
            if not last:
                dve_split(ve, f + 1, 1)
            chain = chained(ve, fin_step, FIN_STEPS * f + 1)
            ve.wait_ge(fin_step, FIN_STEPS * f + 1)
            settle(ve, f)
            for c in range(NC):
                op = ve.bn_aggr(fmv[:, c, :], fst[:, c, :])
            chain(op)
            rsqrt(ve, fmv[:, :, 1], NC, fvs, frstd, frtmp, chain)
            chain(ve.scalar_tensor_tensor(out=fshift[:, :], in0=fmv[:, :, 0], scalar=-1.0, in1=frstd[:, :],
                                          op0=ALU.mult, op1=ALU.mult))

        def dve_fin_out(ve, f):
            for c in range(NC):
                ve.wait_ge(fin_shift, NC * f + c + 1)
                ve.scalar_tensor_tensor(out=x1r[:, c, :], in0=acc[:, c, :], scalar=frstd[:, c:c + 1],
                                        in1=x1r[:, c, :], op0=ALU.mult, op1=ALU.add).then_inc(out_done, 1)

        def dve_hidden(ve, f, t):
            n = NT * f + t
            ve.wait_ge(silu_done, n + 1)
            ve.wait_ge(up_done, n + 1)
            wait(ve, hlo_done, n)
            ve.tensor_tensor(hid[:, :], up_ps[:, :], sg[:, :], ALU.mult).then_inc(gated_done, 1)
            ve.wait_ge(gated_done, n + 1)
            segs = c_segments(t)
            for q in sorted({s[0] for s in segs}):
                ve.wait_ge(row_in[q % 3], 16 * (f * (R // 3) + q // 3 + 1))
            for q, p0, np_ in segs:
                r = slice(p0, p0 + np_)
                op = ve.tensor_tensor(hid[r, :], hid[r, :], crow[r, q % 3, :], ALU.mult)
            op.then_inc(hid_done, 1)

        def dve_body(ve, f, last):
            for t in range(NT):
                n = NT * f + t
                if t and t + AHEAD < NT or t == NT - 1 and not last:
                    dve_split(ve, f, t + AHEAD)
                if t:
                    dve_hidden(ve, f, t)
                if not last:
                    dve_slot(ve, f + 1, 2 * t)
                ve.wait_ge(hhi_done, n + 1)
                ve.tensor_tensor(h_lo[:, t % 2, :], hid[:, :], h_hi[:, t % 2, :].bitcast(F32),
                                 ALU.subtract).then_inc(hlo_done, 1)
                if not last:
                    dve_slot(ve, f + 1, 2 * t + 1)
            if not last:
                dve_xt(ve, f + 1)
            dve_fin_stats(ve, f, last)
            if not last:
                dve_hidden(ve, f + 1, 0)
            dve_fin_out(ve, f)

        block = ctx.enter_context(nc.Block())

        @block.sync
        def _(sp):
            for c in range(NC):
                sp.dma_start(out=xin[:, c, :], in_=x_d[0, c]).then_inc(x0_in, 16)
            for dst, src in ((newton, t_newton), (bqk, b_qk)):
                sp.dma_start(out=dst[:, :], in_=src).then_inc(const_in, 16)
            sp_slot(sp, 0, 0)
            sp.dma_start(out=ident[:, :], in_=t_ident).then_inc(const_in, 16)
            sp.dma_start(out=rw_raw, in_=w_router).then_inc(late_in, 16)
            sp.dma_start(out=bv[:, :], in_=b_v.partition_broadcast(P)).then_inc(late_in, 16)
            sp.dma_start(out=bo[:, :], in_=b_out.partition_broadcast(P)).then_inc(late_in, 16)
            for dst, src in ((mask, t_mask), (dq, t_dq), (dk, t_dk), (lam, t_lam), (blk, t_blk), (rank, t_rank)):
                sp.dma_start(out=dst[tuple([slice(None)] * len(dst.shape))], in_=src).then_inc(late_in, 16)
            for half in (0, 1, 2):
                sp_raw(sp, 0, half // 2, half % 2)
            for s in range(1, 2 * NT):
                if s == FIRST_CHUNK:
                    sp_raw(sp, 0, 1, 1)
                sp_slot(sp, 0, s)
            with sp.Fori(0, NB - 1) as f:
                sp_body(sp, f, False)
            sp_body(sp, NB - 1, True)

        @block.gpsimd
        def _(pool):
            for s in range(2 * NT):
                pool_slot(pool, 0, s)
            for q in range(3):
                pool_row(pool, 0, q)
            pool_body(pool, 0, True, False)
            with pool.Fori(1, NB - 1) as f:
                pool_body(pool, f, False, False)
            pool_body(pool, NB - 1, False, True)
            for c in range(NC):
                pool.wait_ge(out_stored[c], 16 * NB)
            for i in range(2):
                pool.wait_ge(x1_out[i], 16 * NB * NC // 2)
            pool.wait_ge(rows_out, 16 * NB)

        @block.tensor
        def _(pe):
            pe.wait_ge(const_in, 16 * N_CONST)
            for s in range(2 * NT):
                if s == FIRST_CHUNK:
                    pe.wait_ge(const_v, 5)
                    pe.wait_ge(const_a, 1)
                if ("R3",) in SLOTS[s]:
                    pe_gate_up(pe, 0, 0)
                pe_slot(pe, 0, s)
            with pe.Fori(0, NB - 1) as f:
                pe_body(pe, f, False)
            pe_body(pe, NB - 1, True)

        @block.scalar
        def _(act):
            act.wait_ge(const_in, 16 * N_CONST)
            act.wait_ge(const_v, 4)
            for s in range(2 * NT):
                if s == FIRST_CHUNK:
                    act.wait_ge(late_in, 16 * N_LATE)
                    act.copy(rw_hi[:, :], rw_raw).then_inc(const_a, 1)
                    for t in range(2):
                        act_split(act, 0, t)
                act_slot(act, 0, s)
                if ("T2", NC - 1) in SLOTS[s]:
                    act_xt(act, 0)
            act_silu(act, 0, 0)
            with act.Fori(0, NB - 1) as f:
                act_body(act, f, False)
            act_body(act, NB - 1, True)

        @block.vector
        def _(ve):
            ve.memset(qz[:, :, :, :], 0.0).then_inc(const_v, 1)
            ve.memset(state[:, :, :], 0.0).then_inc(const_v, 1)
            ve.memset(sg[:, :], 0.0).then_inc(const_v, 1)
            ve.memset(lgT[:, :], 0.0).then_inc(const_v, 1)
            ve.wait_ge(const_in, 16 * N_CONST)
            for s in range(2 * NT):
                if s == FIRST_CHUNK:
                    ve.wait_ge(late_in, 16 * N_LATE)
                    ve.wait_ge(const_v, 4)
                    ve.wait_ge(const_a, 1)
                    ve.tensor_tensor(rw_lo[:, :], rw_raw, rw_hi[:, :].bitcast(F32),
                                     ALU.subtract).then_inc(const_v, 1)
                    for t in range(2):
                        dve_split(ve, 0, t)
                dve_slot(ve, 0, s)
                if ("T2", NC - 1) in SLOTS[s]:
                    dve_xt(ve, 0)
            dve_hidden(ve, 0, 0)
            with ve.Fori(0, NB - 1) as f:
                dve_body(ve, f, False)
            dve_body(ve, NB - 1, True)


RWW = (KT - 1) * R + P


def decay_tables():
    start = 2.0 ** (-2.0 ** (-(math.log2(HEADS) - 3)))
    slope = np.array([start ** (i + 1) for i in range(HEADS)], np.float32).astype(np.float64)
    pos = np.arange(P)
    diff = pos[None, :] - pos[:, None]
    mask = np.where(diff >= 0, np.exp(-slope[:, None, None] * np.maximum(diff, 0)), 0.0)
    head = np.arange(D) // HD
    dq = np.exp(-slope[head][:, None] * (pos + 1))
    dk = np.exp(-slope[head][None, :] * (P - 1 - pos)[:, None])
    own = (pos[:, None] // HD == pos[None, :] // HD).astype(np.float64)
    lam = np.ascontiguousarray(np.exp(-slope * P)[head].reshape(G, P).T)
    f = np.float32
    return {
        "mask": np.ascontiguousarray(mask.transpose(1, 0, 2)).astype(f),
        "dq": np.ascontiguousarray(dq.reshape(G, P, P).transpose(1, 0, 2)).astype(f),
        "dk": dk.astype(f),
        "lam": lam.astype(f),
        "blk": own.astype(f),
        "ident": np.eye(P, dtype=f),
        "rank": np.tile(np.arange(E, 0, -1, dtype=f), (P, 1)),
        "newton": np.tile(np.array([64, -64, -16, -4], f), (P, 1)),
        "keep": np.repeat(np.where(np.arange(NB) % (SEQ // TOK) == 0, 0, -1).astype(np.int32), P).reshape(NB, P, 1),
    }


def kernel(L0_attn_x, L0_attn_w_qkv, L0_attn_b_qkv, L0_attn_w_out, L0_attn_b_out, L0_ffn_router_weight,
           L0_ffn_gate_up_proj, L0_ffn_down_proj, L0_ffn_sh_gate_w, L0_ffn_sh_up_w, L0_ffn_sh_down_w,
           L0_ffn_shared_gate_w):
    import concourse.bacc as bacc
    from concourse.bass_utils import run_bass_kernel_spmd

    A = np.asarray
    x = A(L0_attn_x)
    wT = A(L0_attn_w_qkv).T
    qk = wT[:, :2 * D].reshape(KT, P, 8, P).transpose(2, 1, 0, 3).reshape(8, P, D)
    w_att = np.concatenate([qk, wT[:, 2 * D:].reshape(KT, P, D), A(L0_attn_w_out).T.reshape(KT, P, D)], 0)
    gu = A(L0_ffn_gate_up_proj)
    gate = np.concatenate([A(L0_ffn_sh_gate_w), gu[:, :I_MOE].reshape(E * I_MOE, D)], 0)
    up = np.concatenate([A(L0_ffn_sh_up_w), gu[:, I_MOE:].reshape(E * I_MOE, D)], 0)
    down = np.concatenate([A(L0_ffn_sh_down_w).T, A(L0_ffn_down_proj).transpose(0, 2, 1).reshape(E * I_MOE, D)], 0)

    def stationary(w):
        return w.reshape(NT, P, KT, P).transpose(0, 3, 2, 1).reshape(NT, P, D)
    w_ffn = np.concatenate([stationary(gate), stationary(up), down.reshape(NT, P, D)], 2)
    w_ffn = w_ffn.reshape(NT, P, 2, UNIT).transpose(0, 2, 1, 3)
    rw = np.concatenate([A(L0_ffn_router_weight), A(L0_ffn_shared_gate_w)], 0)
    w_router = np.zeros((P, RWW), rw.dtype)
    w_router[:, :KT * R] = rw.T.reshape(KT, P, R).transpose(1, 0, 2).reshape(P, KT * R)
    b = A(L0_attn_b_qkv)
    t = decay_tables()
    arrays = {
        "x": x.reshape(-1, D), "w_att": w_att, "w_ffn": w_ffn, "w_router": w_router,
        "b_qk": b[:2 * D].reshape(8, P).T, "b_v": b[2 * D:], "b_out": A(L0_attn_b_out),
        "t_mask": t["mask"], "t_dq": t["dq"], "t_dk": t["dk"], "t_lam": t["lam"], "t_blk": t["blk"],
        "t_ident": t["ident"], "t_rank": t["rank"], "t_newton": t["newton"], "t_keep": t["keep"],
    }
    arrays = {n: np.ascontiguousarray(a) for n, a in arrays.items()}
    nc = bacc.Bacc("TRN2", target_bir_lowering=False, num_devices=1)
    args = {n: nc.dram_tensor(n, list(a.shape), mybir.dt.from_np(a.dtype), kind="ExternalInput").ap()
            for n, a in arrays.items()}
    out = nc.dram_tensor("out", [NB * TOK, D], F32, kind="ExternalOutput").ap()
    build(nc, **args, out=out)
    r = run_bass_kernel_spmd(nc, [arrays], core_ids=[0])
    return r.results[0]["out"].reshape(x.shape)
```
